# Optimizing a Trainium2 kernel written in Bass

```python
import numpy as np
import jax
import jax.numpy as jnp

def _softmax(x, axis=-1):
    return jax.nn.softmax(x, axis=axis)
def _gelu(x):
    return jax.nn.gelu(x, approximate=True)
def _silu(x):
    return jax.nn.silu(x)
def _sigmoid(x):
    return jax.nn.sigmoid(x)
def _layernorm(x, axis=-1, eps=1e-5):
    m = jnp.mean(x, axis=axis, keepdims=True)
    v = jnp.var(x, axis=axis, keepdims=True)
    return (x - m) / jnp.sqrt(v + eps)
def _scatter_add(tgt, idx, src, axis=0):
    return tgt.at[idx].add(src)
def _segment_sum(src, seg, n):
    return jax.ops.segment_sum(src, seg, n)

kernel_name = 'mk_conv_preact_d2_conv_nchw192_644430'

def setup_inputs(seed: int = 0):
    np.random.seed(seed)
    _w = jnp.asarray
    def _rec_inputs():
        import jax
        import jax.numpy as jnp
        _gk = jax.random.key(seed)
        x = -0.0005058 + 1 * jax.random.normal(jax.random.fold_in(_gk, 1), (8, 192, 48, 48), jnp.float32)
        return x
    x = _rec_inputs()
    def _L0_conv_setup():
        import jax, jax.numpy as jnp
        import numpy as np
        B, C, H, W = (8, 192, 48, 48)
        D_EXP = 384
        D_INNER = 384
        K = 4
        N = 16
        R = 12

        def selective_scan(u, delta, A, Bs, Cs, Dskip):
            uT = u.transpose(3, 0, 1, 2)
            dT = delta.transpose(3, 0, 1, 2)
            BT = Bs.transpose(3, 0, 1, 2)
            CT = Cs.transpose(3, 0, 1, 2)
            h0 = jnp.zeros((u.shape[0], K, u.shape[2], A.shape[-1]), u.dtype)

            def step(h, xs_t):
                d_t, u_t, B_t, C_t = xs_t
                dA = jnp.exp(d_t[..., None] * A)
                h = h * dA + (d_t * u_t)[..., None] * B_t[:, :, None, :]
                y = jnp.einsum('bkdn,bkn->bkd', h, C_t)
                return (h, y)
            _, ys = jax.lax.scan(step, h0, (dT, uT, BT, CT))
            ys = ys.transpose(1, 2, 3, 0)
            return ys + u * Dskip[None, :, :, None]
        key = jax.random.key(seed)
        ks = jax.random.split(key, 9)
        return {'x': jax.random.normal(ks[0], (B, C, H, W), jnp.float32), 'in_proj_w': jax.random.normal(ks[1], (2 * D_EXP, C), jnp.float32) * 0.02, 'conv_w': jax.random.normal(ks[2], (D_EXP, 1, 3, 3), jnp.float32) * 0.1, 'conv_b': jax.random.normal(ks[3], (D_EXP,), jnp.float32) * 0.02, 'x_proj_w': jax.random.normal(ks[4], (K, R + 2 * N, D_INNER), jnp.float32) * 0.05, 'dt_w': jax.random.normal(ks[5], (K, D_INNER, R), jnp.float32) * 0.1, 'dt_b': jax.random.normal(ks[6], (K, D_INNER), jnp.float32) * 0.1, 'A_logs': jax.random.uniform(ks[7], (K * D_INNER, N), jnp.float32, -1.0, 1.0), 'Ds': jnp.ones((K * D_INNER,), jnp.float32), 'ln_w': jnp.ones((D_INNER,), jnp.float32), 'ln_b': jnp.zeros((D_INNER,), jnp.float32), 'out_proj_w': jax.random.normal(ks[8], (C, D_EXP), jnp.float32) * 0.02}
    _L0_conv_all = _L0_conv_setup()
    _L0_conv_in = {k: v for k, v in _L0_conv_all.items() if k in ('in_proj_w', 'conv_w', 'conv_b', 'x_proj_w', 'dt_w', 'dt_b', 'A_logs', 'Ds', 'ln_w', 'ln_b', 'out_proj_w', )}
    del _L0_conv_all

    def _L1_conv_setup():
        import jax, jax.numpy as jnp
        import numpy as np
        from jax import lax
        DIM = 192
        HEADS = 4
        EPS = 1e-12

        def _l2norm(t, axis):
            n = jnp.sqrt(jnp.sum(t * t, axis=axis, keepdims=True))
            return t / jnp.maximum(n, EPS)
        key = jax.random.key(seed)
        ks = jax.random.split(key, 8)
        b, c, h, w = (2, DIM, 64, 64)
        x = jax.random.normal(ks[0], (b, c, h, w), dtype=jnp.float32)
        w_qkv = jax.random.normal(ks[1], (3 * c, c), dtype=jnp.float32) * 0.05
        b_qkv = jax.random.normal(ks[2], (3 * c,), dtype=jnp.float32) * 0.05
        w_dw = jax.random.normal(ks[3], (3 * c, 1, 3, 3), dtype=jnp.float32) * 0.05
        b_dw = jax.random.normal(ks[4], (3 * c,), dtype=jnp.float32) * 0.05
        w_proj = jax.random.normal(ks[5], (c, c), dtype=jnp.float32) * 0.05
        b_proj = jax.random.normal(ks[6], (c,), dtype=jnp.float32) * 0.05
        temperature = jnp.ones((HEADS, 1, 1), dtype=jnp.float32)
        return {'x': x, 'w_qkv': w_qkv, 'b_qkv': b_qkv, 'w_dw': w_dw, 'b_dw': b_dw, 'w_proj': w_proj, 'b_proj': b_proj, 'temperature': temperature}
    _L1_conv_all = _L1_conv_setup()
    _L1_conv_in = {k: v for k, v in _L1_conv_all.items() if k in ('w_qkv', 'b_qkv', 'w_dw', 'b_dw', 'w_proj', 'b_proj', 'temperature', )}
    del _L1_conv_all

    return {
        "x": x,
        "L0_conv_in_proj_w": _L0_conv_in["in_proj_w"],
        "L0_conv_conv_w": _L0_conv_in["conv_w"],
        "L0_conv_conv_b": _L0_conv_in["conv_b"],
        "L0_conv_x_proj_w": _L0_conv_in["x_proj_w"],
        "L0_conv_dt_w": _L0_conv_in["dt_w"],
        "L0_conv_dt_b": _L0_conv_in["dt_b"],
        "L0_conv_A_logs": _L0_conv_in["A_logs"],
        "L0_conv_Ds": _L0_conv_in["Ds"],
        "L0_conv_ln_w": _L0_conv_in["ln_w"],
        "L0_conv_ln_b": _L0_conv_in["ln_b"],
        "L0_conv_out_proj_w": _L0_conv_in["out_proj_w"],
        "L1_conv_w_qkv": _L1_conv_in["w_qkv"],
        "L1_conv_b_qkv": _L1_conv_in["b_qkv"],
        "L1_conv_w_dw": _L1_conv_in["w_dw"],
        "L1_conv_b_dw": _L1_conv_in["b_dw"],
        "L1_conv_w_proj": _L1_conv_in["w_proj"],
        "L1_conv_b_proj": _L1_conv_in["b_proj"],
        "L1_conv_temperature": _L1_conv_in["temperature"],
    }

def reference(x, L0_conv_in_proj_w, L0_conv_conv_w, L0_conv_conv_b, L0_conv_x_proj_w, L0_conv_dt_w, L0_conv_dt_b, L0_conv_A_logs, L0_conv_Ds, L0_conv_ln_w, L0_conv_ln_b, L0_conv_out_proj_w, L1_conv_w_qkv, L1_conv_b_qkv, L1_conv_w_dw, L1_conv_b_dw, L1_conv_w_proj, L1_conv_b_proj, L1_conv_temperature):
    import jax
    import jax.numpy as jnp
    def _L0_conv_ref(x, in_proj_w, conv_w, conv_b, x_proj_w, dt_w, dt_b, A_logs, Ds, ln_w, ln_b, out_proj_w):
        import jax, jax.numpy as jnp
        import numpy as np
        B, C, H, W = (8, 192, 48, 48)
        D_EXP = 384
        D_INNER = 384
        K = 4
        N = 16
        R = 12

        def selective_scan(u, delta, A, Bs, Cs, Dskip):
            uT = u.transpose(3, 0, 1, 2)
            dT = delta.transpose(3, 0, 1, 2)
            BT = Bs.transpose(3, 0, 1, 2)
            CT = Cs.transpose(3, 0, 1, 2)
            h0 = jnp.zeros((u.shape[0], K, u.shape[2], A.shape[-1]), u.dtype)

            def step(h, xs_t):
                d_t, u_t, B_t, C_t = xs_t
                dA = jnp.exp(d_t[..., None] * A)
                h = h * dA + (d_t * u_t)[..., None] * B_t[:, :, None, :]
                y = jnp.einsum('bkdn,bkn->bkd', h, C_t)
                return (h, y)
            _, ys = jax.lax.scan(step, h0, (dT, uT, BT, CT))
            ys = ys.transpose(1, 2, 3, 0)
            return ys + u * Dskip[None, :, :, None]
        xz = jnp.einsum('bchw,oc->bohw', x, in_proj_w)
        xx, z = jnp.split(xz, 2, axis=1)
        z1 = jax.nn.gelu(z, approximate=False)
        xx = jax.lax.conv_general_dilated(xx, conv_w, (1, 1), 'SAME', feature_group_count=D_EXP, dimension_numbers=('NCHW', 'OIHW', 'NCHW')) + conv_b[None, :, None, None]
        xx = jax.nn.gelu(xx, approximate=False)
        Bb, Dd, Hh, Ww = xx.shape
        L = Hh * Ww
        x_hw = xx.reshape(Bb, Dd, L)
        x_wh = xx.transpose(0, 1, 3, 2).reshape(Bb, Dd, L)
        xs = jnp.stack([x_hw, x_wh, x_hw[..., ::-1], x_wh[..., ::-1]], axis=1)
        x_dbl = jnp.einsum('bkdl,kcd->bkcl', xs, x_proj_w)
        dts, Bs_, Cs_ = jnp.split(x_dbl, [R, R + N], axis=2)
        dts = jnp.einsum('bkrl,kdr->bkdl', dts, dt_w)
        delta = jax.nn.softplus(dts + dt_b[None, :, :, None])
        A = -jnp.exp(A_logs).reshape(K, D_INNER, N)
        ys = selective_scan(xs, delta, A, Bs_, Cs_, Ds.reshape(K, D_INNER))
        ys = ys[:, 0:2] + ys[:, 2:4, :, ::-1]
        y = ys[:, 0] + ys[:, 1].reshape(Bb, Dd, Ww, Hh).transpose(0, 1, 3, 2).reshape(Bb, Dd, L)
        y = y.transpose(0, 2, 1)
        mu = y.mean(-1, keepdims=True)
        var = ((y - mu) ** 2).mean(-1, keepdims=True)
        y = (y - mu) / jnp.sqrt(var + 1e-05) * ln_w + ln_b
        y = y.reshape(Bb, Hh, Ww, Dd).transpose(0, 3, 1, 2)
        y = y * z1
        out = jnp.einsum('bdhw,cd->bchw', y, out_proj_w)
        return out

    def _L1_conv_ref(x, w_qkv, b_qkv, w_dw, b_dw, w_proj, b_proj, temperature):
        import jax, jax.numpy as jnp
        import numpy as np
        from jax import lax
        DIM = 192
        HEADS = 4
        EPS = 1e-12

        def _l2norm(t, axis):
            n = jnp.sqrt(jnp.sum(t * t, axis=axis, keepdims=True))
            return t / jnp.maximum(n, EPS)
        b, c, h, w = x.shape
        heads = temperature.shape[0]
        hd = c // heads
        qkv = jnp.einsum('bchw,oc->bohw', x, w_qkv) + b_qkv[None, :, None, None]
        qkv = lax.conv_general_dilated(qkv, w_dw, window_strides=(1, 1), padding=((1, 1), (1, 1)), dimension_numbers=('NCHW', 'OIHW', 'NCHW'), feature_group_count=3 * c) + b_dw[None, :, None, None]
        q, k, v = jnp.split(qkv, 3, axis=1)
        q = q.reshape(b, heads, hd, h * w)
        k = k.reshape(b, heads, hd, h * w)
        v = v.reshape(b, heads, hd, h * w)
        q = _l2norm(q, axis=2)
        k = _l2norm(k, axis=2)
        attn = jnp.einsum('bhdn,bhdm->bhnm', q, k) * temperature[None]
        attn = jax.nn.softmax(attn, axis=-1)
        out = jnp.einsum('bhnm,bhdm->bhdn', attn, v)
        out = out.reshape(b, c, h, w)
        out = jnp.einsum('bchw,oc->bohw', out, w_proj) + b_proj[None, :, None, None]
        return out

    def _gn(v, G=32, eps=1e-5):
        B_, C_, H_, W_ = v.shape
        g = v.reshape(B_, G, C_ // G, H_, W_)
        m = jnp.mean(g, axis=(2, 3, 4), keepdims=True)
        s = jnp.var(g, axis=(2, 3, 4), keepdims=True)
        return ((g - m) / jnp.sqrt(s + eps)).reshape(v.shape)

    def _ln_c(v, eps=1e-6):
        m = jnp.mean(v, axis=1, keepdims=True)
        s = jnp.var(v, axis=1, keepdims=True)
        return (v - m) / jnp.sqrt(s + eps)

    def _ln_t(v, eps=1e-5):
        m = jnp.mean(v, axis=-1, keepdims=True)
        s = jnp.var(v, axis=-1, keepdims=True)
        return (v - m) / jnp.sqrt(s + eps)

    def _to_tokens(v):
        B_, C_, H_, W_ = v.shape
        return v.reshape(B_, C_, H_ * W_).transpose(0, 2, 1)
    def _from_tokens(t, like):
        B_, C_, H_, W_ = like.shape
        return t.transpose(0, 2, 1).reshape(B_, C_, H_, W_)

    x = x + _L0_conv_ref(_gn(x), L0_conv_in_proj_w, L0_conv_conv_w, L0_conv_conv_b, L0_conv_x_proj_w, L0_conv_dt_w, L0_conv_dt_b, L0_conv_A_logs, L0_conv_Ds, L0_conv_ln_w, L0_conv_ln_b, L0_conv_out_proj_w)
    x = x + _L1_conv_ref(_gn(x), L1_conv_w_qkv, L1_conv_b_qkv, L1_conv_w_dw, L1_conv_b_dw, L1_conv_w_proj, L1_conv_b_proj, L1_conv_temperature)
    return x


_drawn_inputs = setup_inputs


def setup_inputs(seed=0):
    import zlib

    import numpy as np

    out = dict(_drawn_inputs(seed))
    spreads = {'L0_conv_Ds': (1.0, 0.6),
     'L0_conv_ln_w': (1.0, 0.6),
     'L0_conv_ln_b': (0.0, 0.8),
     'L1_conv_temperature': (1.0, 0.6)}
    factors = {'L0_conv_conv_b': 4.349,
     'L0_conv_x_proj_w': 8.0,
     'L0_conv_dt_w': 8.0,
     'L0_conv_dt_b': 8.0,
     'L0_conv_A_logs': 8.0,
     'L1_conv_w_qkv': 8.0,
     'L1_conv_b_qkv': 8.0,
     'L1_conv_w_dw': 8.0}
    for name, (base, spread) in spreads.items():
        noise = np.random.default_rng([zlib.crc32(name.encode()), seed]).standard_normal(out[name].shape)
        drawn = base * np.exp(spread * noise) if base else spread * noise
        out[name] = jnp.asarray(drawn.astype(out[name].dtype))
    for name, factor in factors.items():
        out[name] = (out[name] * factor).astype(out[name].dtype)
    return out
```

```python
from contextlib import ExitStack

import numpy as np
import concourse.bass as bass
from concourse import mybir

F32 = mybir.dt.float32
BF16 = mybir.dt.bfloat16
ALU = mybir.AluOpType
ACT = mybir.ActivationFunctionType
ds = bass.ds

NB, C, H, W = 8, 192, 48, 48
L = H * W
CP = 96
CT = C // CP
DI = 384
J = DI // 128
K, N, R = 4, 16, 12
CH = 8 * W
NC = L // CH
HP = H + 2
PAD = HP * HP
JC = J * CH
HEADS, HD = 4, 48
PAIRS = HEADS // 2
MT = L // 128
QC = 2 * CH
QT = 6
GN_OPS = 22
LN65536 = 16.0 * float(np.log(2.0))

U = 0
DTS = U + 2 * J * L
DT0 = (64, 0, 96, 32)
BC = DTS + L
Y = BC + K * L // 2
XS = Y + J * L
DEL, DU, DBU, HC, HB = (XS + 2 * i * JC for i in range(5))
NH = 4
BS = HB + NH * JC
SCAN_END = BS + 2 * CH
XPAD = Y
X = XPAD + J * PAD + 4
XN = X + CT * L + 160
RES = XN + CT * L
Z = J * L
SQ = 0
Q = 0
KZ = Q + PAIRS * L
V = KZ + HEADS * L
VT = V + PAIRS * L
XP2 = VT + MT * PAIRS * 128
XP2C = XN + CT * L + 8
PB = XN
AREA = max(XP2C + PAD + 4, SCAN_END)
assert XP2 + 2 * PAD <= X and SCAN_END <= AREA and RES + 8 * CH <= AREA


def build(nc, t, out):
    ctx = ExitStack()
    with ctx:
        def sb(name, shape, dt=F32):
            return ctx.enter_context(nc.sbuf_tensor(name, shape, dt))

        def sem(name):
            return ctx.enter_context(nc.semaphore(name))

        w_in = sb("w_in", [CP, CT, 2 * DI])
        w_xp = sb("w_xp", [128, J, 2, 128])
        w_dt = sb("w_dt", [128, K, DI])
        ident = sb("ident", [128, 128])
        sel = sb("sel", [96, 2 * N, 128], BF16)
        a_neg = sb("a_neg", [128, J, K, N])
        d_skip = sb("d_skip", [128, J, K])
        d_sum = sb("d_sum", [128, J, 2])
        w_cv = sb("w_cv", [128, J, 9])
        b_cv = sb("b_cv", [128, J])
        b_dt = sb("b_dt", [128, J, K])
        ln_w = sb("ln_w", [128, J])
        ln_b = sb("ln_b", [128, J])
        w_out = sb("w_out", [128, J, C])
        gmat = sb("gmat", [CP, CP])
        mean_m = sb("mean_m", [128, 128])
        w_qkv = sb("w_qkv", [CP, CT, QT * 128])
        b_qkv = sb("b_qkv", [128, QT])
        w_dw = sb("w_dw", [128, QT, 9])
        b_dw = sb("b_dw", [128, QT])
        w_pr = sb("w_pr", [128, PAIRS, C])
        b_pr = sb("b_pr", [CP, CT])
        t_q = sb("t_q", [128, PAIRS])
        t_all = sb("t_all", [128, HEADS])
        t_neg = sb("t_neg", [128, HEADS])
        hones = sb("hones", [128, 128])
        hind = sb("hind", [128, 2])
        ssel = sb("ssel", [128, 2])
        eps5 = sb("eps5", [128, 1])
        ones = sb("ones", [128, 1])
        ln_shift = sb("ln_shift", [128, 1])
        hst = sb("hst", [128, N, J])
        gst = sb("gst", [CP, CT, 6, 6])
        gmv = sb("gmv", [CP, CT, 2])
        gdm = sb("gdm", [CP, CT])
        gd2 = sb("gd2", [CP, CT])
        gq = sb("gq", [CP, CT])
        gmean = sb("gmean", [CP, CT])
        gstd = sb("gstd", [CP, CT])
        grs = sb("grs", [CP, 2, CT])
        gnb = sb("gnb", [CP, 2, CT])
        kn = sb("kn", [128, PAIRS, 2 * MT])
        ksc = sb("ksc", [128, PAIRS, 2 * MT])
        area = sb("area", [128, AREA])
        ps = ctx.enter_context(nc.psum_tensor("ps", [128, 8, 512], F32))

        def ar(off, n, p0=0, p1=128):
            return area[p0:p1, off:off + n]

        u_v = ar(U, 2 * J * L).rearrange("p (o j l) -> p o j l", o=2, j=J)
        dts = ar(DTS, L)
        bc = area[0:96, BC:BC + K * L // 2].bitcast(BF16).rearrange("p (k l) -> p k l", k=K)
        y_v = ar(Y, J * L).rearrange("p (j l) -> p j l", j=J)
        dlt = ar(DEL, 2 * JC).rearrange("p (b j l) -> p b j l", b=2, j=J)
        du = ar(DU, 2 * JC).rearrange("p (b j l) -> p b j l", b=2, j=J)
        dbu = ar(DBU, 2 * JC).rearrange("p (b j l) -> p b j l", b=2, j=J)
        hb = ar(HB, NH * JC).rearrange("p (b j l) -> p b j l", b=NH, j=J)
        hc = ar(HC, 2 * JC).rearrange("p (b j l) -> p b j l", b=2, j=J)
        bs = ar(BS, 2 * CH).rearrange("p (b l) -> p b l", b=2)
        xpad = ar(XPAD, J * PAD).rearrange("p (j h w) -> p j h w", j=J, h=HP)
        x_v = ar(X, CT * L, 0, CP).rearrange("p (t l) -> p t l", t=CT)
        xn = ar(XN, CT * L, 0, CP).rearrange("p (t l) -> p t l", t=CT)
        res = ar(RES, 8 * CH).rearrange("p (q a l) -> p q a l", q=4, a=2)
        z_v = ar(Z, J * L).rearrange("p (j l) -> p j l", j=J)
        sq_v = ar(SQ, J * L).rearrange("p (j l) -> p j l", j=J)
        q_v = ar(Q, PAIRS * L).rearrange("p (i l) -> p i l", i=PAIRS)
        kz = ar(KZ, HEADS * L).rearrange("p (i l) -> p i l", i=HEADS)
        v_v = ar(V, PAIRS * L).rearrange("p (i l) -> p i l", i=PAIRS)
        vt = ar(VT, MT * PAIRS * 128).rearrange("p (m i c) -> p m i c", m=MT, i=PAIRS)
        xp2 = [ar(o, PAD).rearrange("p (h w) -> p h w", h=HP) for o in (XP2, XP2 + PAD, XP2C)]
        pb = ar(PB, 4 * QC).rearrange("p (b l) -> p b l", b=4)
        sqq = [ar(XN, L), ar(XP2, L)]
        sqk = [ar(XN + L, L), ar(XP2 + PAD, L)]
        spread = ar(KZ, PAIRS * L).rearrange("p (i m c) -> p i m c", i=PAIRS, m=MT)

        consts = sem("consts")
        prepared = sem("prepared")
        exp_a = sem("exp_a")
        phase = sem("phase")
        passed = sem("passed")
        x_in = sem("x_in")
        stored = sem("stored")
        gn_v = sem("gn_v")
        gn_p = sem("gn_p")
        gn_a = sem("gn_a")
        in_mm = sem("in_mm")
        in_ev = sem("in_ev")
        pad0 = sem("pad0")
        conv = sem("conv")
        gel = sem("gel")
        xp_mm = sem("xp_mm")
        xp_ev = sem("xp_ev")
        xp_sp = sem("xp_sp")
        b_mm = sem("b_mm")
        b_sb = sem("b_sb")
        c_mm = sem("c_mm")
        da = sem("da")
        scan = sem("scan")
        dbus = sem("dbus")
        carry = sem("carry")
        hcs = sem("hcs")
        ysum = sem("ysum")
        yev = sem("yev")
        dp_mm = sem("dp_mm")
        dp_rd = sem("dp_rd")
        dp_a = sem("dp_a")
        dp_v = sem("dp_v")
        z_mm = sem("z_mm")
        z_ge = sem("z_ge")
        mu_mm = sem("mu_mm")
        cen = sem("cen")
        sqs = sem("sqs")
        var_mm = sem("var_mm")
        rsd = sem("rsd")
        nrm = sem("nrm")
        o_mm = sem("o_mm")
        x1s = sem("x1s")
        qk_mm = sem("qk_mm")
        qk_ev = sem("qk_ev")
        cv2 = sem("cv2")
        kclr = sem("kclr")
        qsq = sem("qsq")
        n_mm = sem("n_mm")
        n_cl = sem("n_cl")
        n_ac = sem("n_ac")
        k_ac = sem("k_ac")
        k_v = sem("k_v")
        qn = sem("qn")
        kzs = sem("kzs")
        vt_mm = sem("vt_mm")
        vt_ev = sem("vt_ev")
        s_mm = sem("s_mm")
        ex = sem("ex")
        pv = sem("pv")
        o_ev = sem("o_ev")
        r_mm = sem("r_mm")
        r_v = sem("r_v")
        on = sem("on")
        p_mm = sem("p_mm")
        x2s = sem("x2s")

        loads = [
            (w_in[:], t["w_in"]), (w_xp[:], t["w_xp"]), (w_dt[:], t["w_dt"]),
            (ident[:], t["ident"]), (a_neg[:], t["a_logs"]), (d_skip[:], t["ds"]), (w_cv[:], t["w_cv"]),
            (b_cv[:], t["b_cv"]), (b_dt[:], t["b_dt"]), (ln_w[:], t["ln_w"]), (ln_b[:], t["ln_b"]),
            (w_out[:], t["w_out"]), (gmat[:], t["gmat"]), (mean_m[:], t["mean_m"]), (w_qkv[:], t["w_qkv"]),
            (b_qkv[:], t["b_qkv"]), (w_dw[:], t["w_dw"]), (b_dw[:], t["b_dw"]), (w_pr[:], t["w_pr"]),
            (b_pr[:], t["b_pr"]), (t_q[:], t["t_q"]), (t_all[:], t["t_all"]), (hones[:], t["hones"]),
            (hind[:], t["hind"]), (ssel[:], t["ssel"]),
            (area[0:96, 0:2 * N * 128], t["sel"]),
        ]

        block = ctx.enter_context(nc.Block())

        def alone(e):
            e.sem_inc(passed, 1)

        def barrier(e, b, i):
            alone(e)
            e.drain().then_inc(phase, 1)
            e.wait_ge(phase, b * 16 + 4 * (i + 1))

        def wait_stored(e, b):
            e.wait_ge(stored, b * 16 + 16)

        def walk(e, body):
            for k in range(K):
                last, nxt = ((k - 1, NC - 1) if k else None), ((k + 1, 0) if k < K - 1 else None)
                body(k, 0, 0, last, (k, 1))
                with e.Fori(0, 2) as cc:
                    c = e.snap(2 * cc)
                    body(k, c + 1, 1, (k, c), (k, c + 2))
                    body(k, c + 2, 0, (k, c + 1), (k, c + 3))
                body(k, NC - 1, 1, (k, NC - 2), nxt)

        def pos(k, c):
            return c * CH if k < 2 else (NC - 1) * CH - c * CH

        def rev(ap, k):
            return ap if k < 2 else ap[:, ::-1]

        ps3 = ps[:, 2:5, 0:CH]
        py3 = ps[:, 5:8, 0:CH]

        @block.sync
        def _(e):
            for dst, src in loads:
                e.dma_start(dst, src).then_inc(consts, 16)
            e.wait_ge(prepared, 8)
            with e.Fori(0, NB) as b:
                xb = t["x"][ds(b, 1)].rearrange("o (t p) l -> p (o t) l", p=CP)
                e.dma_start(x_v, xb).then_inc(x_in, 16)
                e.wait_ge(phase, b * 16 + 8)
                e.dma_start(x_v, xb).then_inc(x_in, 16)
                e.wait_ge(x2s, b * 12 + 16)
                e.dma_start(out[ds(b, 1)].rearrange("o (t p) l -> p (o t) l", p=CP), x_v).then_inc(stored, 16)
                e.wait_ge(stored, b * 16 + 16)
                e.wait_ge(phase, b * 16 + 16)
                alone(e)
            e.wait_ge(stored, NB * 16)

        @block.tensor
        def _(e):
            e.wait_ge(consts, 16 * len(loads))
            e.wait_ge(prepared, 8)

            def group_sums(b, q):
                g = b * 2 + q
                e.wait_ge(gn_v, g * GN_OPS + 14)
                e.matmul(ps[0:CP, 7, 0:CT], gmat[:], gmv[:, :, 0], start=True, stop=True).then_inc(gn_p, 1)
                e.wait_ge(gn_v, g * GN_OPS + 18)
                e.matmul(ps[0:CP, 7, 8:8 + CT], gmat[:], gq[:], start=True, stop=True).then_inc(gn_p, 1)

            def front(b):
                group_sums(b, 0)
                e.wait_ge(gn_v, b * 2 * GN_OPS + GN_OPS)
                alone(e)
                for j in range(J):
                    with e.Fori(0, 3) as cc:
                        for s in range(2):
                            e.wait_ge(in_ev, b * 18 + cc * 2 + (6 * j + s + 1))
                            for k in range(CT):
                                m = e.matmul(ps[:, 4 + s, 0:CH], w_in[:, k, j * 128:(j + 1) * 128],
                                             xn[:, k, ds(cc * 2 * CH + s * CH, CH)], start=k == 0, stop=k == CT - 1)
                            m.then_inc(in_mm, 1)
                e.wait_ge(gel, b * 6 + 6)
                alone(e)
                with e.Fori(0, 3) as cc:
                    for s in range(2):
                        for o in range(2):
                            q = 2 * s + o
                            e.wait_ge(xp_sp, b * 48 + cc * 16 + (4 * q + 2))
                            for j in range(J):
                                m = e.matmul(ps[:, q, 0:CH], w_xp[:, j, o], u_v[:, o, j, ds(cc * 2 * CH + s * CH, CH)],
                                             start=j == 0, stop=j == J - 1)
                            m.then_inc(xp_mm, 1)

            def scan_phase(b):
                def delta_tile(k, c, j):
                    e.matmul(ps[:, 0, 0:CH], w_dt[:, k, j * 128:(j + 1) * 128], dts[:, ds(pos(k, c), CH)],
                             start=True, stop=True).then_inc(dp_mm, 1)

                def b_row(k, c, n):
                    e.matmul(ps[:, 0, 0:CH], sel[:, n], bc[:, k, ds(pos(k, c), CH)],
                             start=True, stop=True).then_inc(b_mm, 1)

                def c_row(k, c, n):
                    e.matmul(ps[:, 1, 0:CH], sel[:, N + n], bc[:, k, ds(pos(k, c), CH)],
                             start=True, stop=True).then_inc(c_mm, 1)

                c_row(0, 0, 0)
                for j in range(J):
                    if j:
                        e.wait_ge(dp_rd, b * 72 + j)
                    delta_tile(0, 0, j)
                for n in range(4):
                    if n == 0:
                        e.wait_ge(dp_rd, b * 72 + 3)
                    else:
                        e.wait_ge(b_sb, b * 384 + n)
                    b_row(0, 0, n)

                def body(k, c, par, last, nxt):
                    g = e.snap(b * 24 + (c + k * NC))
                    g16, g3 = e.snap(g * 16), e.snap(g * 3)
                    for i in range(N):
                        e.wait_ge(hcs, g16 + (i + 2))
                        if i < N - 1 or nxt:
                            c_row(*((k, c, i + 1) if i < N - 1 else (*nxt, 0)))
                        if i < N - 4 or nxt:
                            if nxt and i in (1, 3, 5):
                                e.wait_ge(dp_rd, g3 + (4 + i // 2))
                            else:
                                e.wait_ge(b_sb, g16 + (i + 4))
                            b_row(*((k, c, i + 4) if i < N - 4 else (*nxt, i + 4 - N)))
                        if i == 0:
                            e.wait_ge(yev, g + 1)
                        for j in range(J):
                            m = e.matmul(ps[:, 5 + j, 0:CH], ident[:], hc[:, i % 2, j], start=i == 0, stop=i == N - 1)
                            if nxt and i in (0, 2, 4) and j == 0:
                                e.wait_ge(b_sb, g16 + (i + 5))
                                delta_tile(*nxt, i // 2)
                        m.then_inc(ysum, 1)

                walk(e, body)

            def back(b):
                e.wait_ge(nrm, b * 32 + 12)
                alone(e)
                with e.Fori(0, 3) as cc:
                    for s in range(2):
                        for j in range(J):
                            e.wait_ge(z_ge, b * 18 + cc * 6 + (3 * s + j + 1))
                            for k in range(CT):
                                m = e.matmul(ps[:, 3 * s + j, 0:CH], w_in[:, k, DI + j * 128:DI + (j + 1) * 128],
                                             xn[:, k, ds(cc * 2 * CH + s * CH, CH)], start=k == 0, stop=k == CT - 1)
                            m.then_inc(z_mm, 1)
                with e.Fori(0, 3) as cc:
                    for s in range(2):
                        e.wait_ge(cen, b * 6 + cc * 2 + (s + 1))
                        for j in range(J):
                            m = e.matmul(ps[:, 6 + s, 0:CH], mean_m[:], y_v[:, j, ds(cc * 2 * CH + s * CH, CH)],
                                         start=j == 0, stop=j == J - 1)
                        m.then_inc(mu_mm, 1)
                e.wait_ge(z_ge, b * 18 + 24)
                alone(e)
                with e.Fori(0, 3) as cc:
                    for s in range(2):
                        e.wait_ge(sqs, b * 6 + cc * 2 + (s + 1))
                        e.wait_ge(nrm, b * 32 + cc * 10 + (5 * s + 3))
                        for j in range(J):
                            m = e.matmul(ps[:, s, 0:CH], mean_m[:], sq_v[:, j, ds(cc * 2 * CH + s * CH, CH)],
                                         start=j == 0, stop=j == J - 1)
                        m.then_inc(var_mm, 1)
                with e.Fori(0, 3) as cc:
                    for s in range(2):
                        e.wait_ge(nrm, b * 32 + cc * 10 + (5 * s + 17))
                        for h in range(CT):
                            e.wait_ge(x1s, b * 12 + cc * 4 + (2 * s + h + 1))
                            for j in range(J):
                                m = e.matmul(ps[0:CP, 2 + 2 * s + h, 0:CH], w_out[:, j, h * CP:(h + 1) * CP],
                                             y_v[:, j, ds(cc * 2 * CH + s * CH, CH)], start=j == 0, stop=j == J - 1)
                            m.then_inc(o_mm, 1)

            def attention(b):
                group_sums(b, 1)
                e.wait_ge(gn_v, b * 2 * GN_OPS + 2 * GN_OPS)
                alone(e)
                for i in range(QT):
                    with e.Fori(0, 3) as cc:
                        for s in range(2):
                            e.wait_ge(qk_ev, b * 36 + cc * 2 + (6 * i + s + 1))
                            for k in range(CT):
                                m = e.matmul(ps[:, 6 + s, 0:CH], w_qkv[:, k, i * 128:(i + 1) * 128],
                                             xn[:, k, ds(cc * 2 * CH + s * CH, CH)], start=k == 0, stop=k == CT - 1)
                            m.then_inc(qk_mm, 1)
                e.wait_ge(qk_ev, b * 36 + 36 + 2)
                for p in range(PAIRS):
                    e.wait_ge(cv2, b * 108 + (54 * p + 54))
                    for g in range(5):
                        if g >= 2:
                            e.wait_ge(vt_ev, b * 10 + (5 * p + g - 1))
                        for m in range(4 * g, min(4 * g + 4, MT)):
                            i = e.matmul(ps[:, 3 + g % 2, (m % 4) * 128:(m % 4) * 128 + 128],
                                         v_v[:, p, m * 128:(m + 1) * 128], ident[:], start=True, stop=True)
                        i.then_inc(vt_mm, 1)
                    e.wait_ge(qsq, b * 4 + 2 * p + 1)
                    for c in range(NC):
                        e.wait_ge(qn, b * 12 + (6 * p + c + 1))
                        e.matmul(ps[:, c % 2, 0:CH], hones[:], sqq[p][:, c * CH:(c + 1) * CH],
                                 start=True, stop=True).then_inc(n_mm, 1)
                    e.wait_ge(qsq, b * 4 + 2 * p + 2)
                    for m in range(MT):
                        i = e.matmul(ps[:, 2, 2 * m:2 * m + 2], sqk[p][:, m * 128:(m + 1) * 128], hind[:],
                                     start=True, stop=True)
                    i.then_inc(n_mm, 1)
                    e.wait_ge(vt_ev, b * 10 + (5 * p + 5))
                    e.wait_ge(qn, b * 12 + (6 * p + 6 + 2))
                    e.wait_ge(kzs, b * 4 + (2 * p + 2))
                    e.wait_ge(k_ac, b * 2 + (p + 1))
                    alone(e)
                    with e.Fori(0, 3) as c:
                        turn = e.snap(b * 6 + c + 3 * p)
                        base = e.snap(turn * 36)

                        def scores(w):
                            m, h = divmod(w, 2)
                            e.wait_ge(ex, base + (w + 1))
                            for s in range(2):
                                i = e.matmul(ps[:, 2 * (w % 3) + s, 0:CH], kz[:, 2 * p + h, m * 128:(m + 1) * 128],
                                             q_v[:, p, ds(c * QC + s * CH, CH)], start=True, stop=True)
                            i.then_inc(s_mm, 1)

                        def values(w):
                            m, h = divmod(w, 2)
                            e.wait_ge(ex, base + (w + 4))
                            if w == 0:
                                e.wait_ge(o_ev, turn + 1)
                            for s in range(2):
                                i = e.matmul(ps[64 * h:64 * h + 64, 6 + s, 0:CH], vt[:, m, p, 64 * h:64 * h + 64],
                                             pb[:, w % 4, s * CH:(s + 1) * CH], start=m == 0, stop=m == MT - 1)
                            i.then_inc(pv, 1)

                        scores(0)
                        scores(1)
                        for m in range(MT):
                            for w in (2 * m + 2, 2 * m + 3):
                                if w < 2 * MT:
                                    scores(w)
                            values(2 * m)
                            values(2 * m + 1)
                for p in range(PAIRS):
                    e.wait_ge(o_ev, b * 6 + (3 * p + 3 + 1))
                    for m in range(MT):
                        i = e.matmul(ps[:, p, 2 * m:2 * m + 2], q_v[:, p, m * 128:(m + 1) * 128], ssel[:],
                                     start=True, stop=True)
                    i.then_inc(r_mm, 1)
                for p in range(PAIRS):
                    e.wait_ge(r_v, b * 4 + (2 * p + 2))
                    for g in range(5):
                        q = 5 * p + g
                        if q >= 2:
                            e.wait_ge(on, b * 10 + (q - 1))
                        for m in range(4 * g, min(4 * g + 4, MT)):
                            i = e.matmul(ps[:, 2 + q % 2, (m % 4) * 128:(m % 4) * 128 + 128],
                                         spread[:, p, m], ident[:], start=True, stop=True)
                        i.then_inc(r_mm, 1)
                e.wait_ge(on, b * 10 + 10)
                alone(e)
                with e.Fori(0, 3) as cc:
                    for s in range(2):
                        for h in range(CT):
                            e.wait_ge(x2s, b * 12 + cc * 4 + (2 * s + h + 1))
                            for p in range(PAIRS):
                                m = e.matmul(ps[0:CP, 2 + 2 * s + h, 0:CH], w_pr[:, p, h * CP:(h + 1) * CP],
                                             q_v[:, p, ds(cc * 2 * CH + s * CH, CH)], start=p == 0, stop=p == PAIRS - 1)
                            m.then_inc(p_mm, 1)

            with e.Fori(0, NB) as b:
                for i, f in enumerate((front, scan_phase, back, attention)):
                    f(b)
                    barrier(e, b, i)
                wait_stored(e, b)

        @block.vector
        def _(e):
            e.memset(ones[:], 1.0).then_inc(prepared, 1)
            e.memset(eps5[:], 1e-5).then_inc(prepared, 1)
            e.memset(ln_shift[:], 0.5 * LN65536).then_inc(prepared, 1)
            e.wait_ge(consts, 16 * len(loads))
            e.tensor_copy(sel[:].rearrange("p n m -> p (n m)"), area[0:96, 0:2 * N * 128]).then_inc(prepared, 1)
            e.scalar_tensor_tensor(out=t_neg[:], in0=t_all[:], scalar=-1.0, in1=t_all[:],
                                   op0=ALU.mult, op1=ALU.min).then_inc(prepared, 1)
            e.tensor_tensor(d_sum[:], d_skip[:, :, 0:2], d_skip[:, :, 2:4], ALU.add).then_inc(prepared, 1)
            e.wait_ge(prepared, 6)
            e.tensor_tensor(d_sum[:, :, 0], d_sum[:, :, 0], d_sum[:, :, 1], ALU.add).then_inc(prepared, 1)
            e.wait_ge(exp_a, 1)
            e.tensor_scalar(a_neg[:], a_neg[:], -1.0, None, ALU.mult).then_inc(prepared, 1)
            for s, v in ((xp_sp, 16), (scan, 3), (hcs, 1), (yev, 1), (cen, 2), (x1s, 4), (x2s, 4), (qn, 2), (nrm, 10)):
                e.sem_inc(s, v)
            e.wait_ge(prepared, 8)

            def groupnorm(b, q):
                g = e.snap((b * 2 + q) * GN_OPS)
                for k in range(CT):
                    for i in range(6):
                        e.bn_stats(gst[:, k, i], x_v[:, k, i * CH:(i + 1) * CH]).then_inc(gn_v, 1)
                e.wait_ge(gn_v, g + 12)
                alone(e)
                for k in range(CT):
                    e.bn_aggr(gmv[:, k], gst[:, k].rearrange("p a c -> p (a c)")).then_inc(gn_v, 1)
                e.wait_ge(gn_v, g + 14)
                e.wait_ge(gn_p, b * 4 + (2 * q + 1))
                e.tensor_tensor(gdm[:], gmv[:, :, 0], ps[0:CP, 7, 0:CT], ALU.subtract).then_inc(gn_v, 1)
                e.tensor_copy(gmean[:], ps[0:CP, 7, 0:CT]).then_inc(gn_v, 1)
                e.wait_ge(gn_v, g + 16)
                e.tensor_tensor(gd2[:], gdm[:], gdm[:], ALU.mult).then_inc(gn_v, 1)
                e.wait_ge(gn_v, g + 17)
                e.tensor_tensor(gq[:], gd2[:], gmv[:, :, 1], ALU.add).then_inc(gn_v, 1)
                e.wait_ge(gn_a, b * 2 + (q + 1))
                e.reciprocal(grs[:, q], gstd[:]).then_inc(gn_v, 1)
                e.wait_ge(gn_v, g + 19)
                e.scalar_tensor_tensor(out=gnb[:, q], in0=gmean[:], scalar=-1.0, in1=grs[:, q],
                                       op0=ALU.mult, op1=ALU.mult).then_inc(gn_v, 1)
                e.wait_ge(gn_v, g + 20)
                normalise(q, gn_v)

            def normalise(q, done):
                for k in range(CT):
                    e.tensor_scalar(xn[:, k], x_v[:, k], grs[:, q, k:k + 1], gnb[:, q, k:k + 1],
                                    ALU.mult, ALU.add).then_inc(done, 1)

            def conv_taps(base, i, done, src, dst, w, bias):
                base = e.snap(base + 18 * i)
                acc = dst.rearrange("p (h w) -> p h w", h=H)
                for tap in range(9):
                    dy, dx = divmod(tap, 3)
                    for half in range(2):
                        r = 24 * half
                        a, x = acc[:, r:r + 24], src[:, r + dy:r + dy + 24, dx:dx + W]
                        if tap == 0:
                            e.tensor_scalar(a, x, w[:, i, 0:1], bias[:, i:i + 1], ALU.mult, ALU.add).then_inc(done, 1)
                        else:
                            e.wait_ge(done, base + (2 * tap - 1 + half))
                            e.scalar_tensor_tensor(out=a, in0=x, scalar=w[:, i, tap:tap + 1], in1=a,
                                                   op0=ALU.mult, op1=ALU.add).then_inc(done, 1)

            def front(b):
                e.wait_ge(x_in, b * 32 + 16)
                groupnorm(b, 0)
                e.wait_ge(pad0, b + 1)
                for j in range(J):
                    e.wait_ge(in_ev, b * 18 + (6 * j + 6 + 2))
                    conv_taps(b * 54, j, conv, xpad[:, j], u_v[:, 0, j], w_cv, b_cv)
                with e.Fori(0, 3) as cc:
                    for s in range(2):
                        for o in range(2):
                            q = 2 * s + o
                            done = e.snap(b * 48 + cc * 16 + (4 * q + 16))
                            part = bc[:, o:K:2, ds(cc * 2 * CH + s * CH, CH)]
                            for a in range(2):
                                e.wait_ge(xp_ev, b * 36 + cc * 12 + (3 * q + 2 + a))
                                e.tensor_tensor(res[0:32, q, a], ps[32 * a:32 * a + 32, q, 0:CH], part[64:96, a],
                                                ALU.subtract).then_inc(xp_sp, 1)
                            e.wait_ge(xp_sp, done + 2)
                            e.tensor_copy(part[0:32], res[0:32, q]).then_inc(xp_sp, 1)
                            e.wait_ge(xp_sp, done + 3)
                            e.tensor_tensor(part[32:64], res[0:32, q], part[0:32], ALU.subtract).then_inc(xp_sp, 1)

            def scan_phase(b):
                def delta(g, par, k, c, v):
                    e.wait_ge(dp_a, g * 9 + 9)
                    e.scalar_tensor_tensor(out=dlt[:, par], in0=dlt[:, par], scalar=0.0, in1=du[:, par],
                                           op0=ALU.max, op1=ALU.add).then_inc(dp_v, 1)
                    e.wait_ge(dp_v, v + 1)
                    e.tensor_tensor(du[:, par], dlt[:, par], u_v[:, k % 2, :, ds(pos(k, c), CH)], ALU.mult)\
                        .then_inc(dp_v, 1)

                def add_y(k, c):
                    if k == 0:
                        for j in range(J):
                            m = e.scalar_tensor_tensor(out=y_v[:, j, ds(pos(k, c), CH)], in0=u_v[:, 0, j, ds(pos(k, c), CH)],
                                                       scalar=d_sum[:, j, 0:1], in1=ps[:, 5 + j, 0:CH],
                                                       op0=ALU.mult, op1=ALU.add)
                    elif k % 2 == 0:
                        o = y_v[:, :, ds(pos(k, c), CH)]
                        m = e.tensor_tensor(o, o, py3, ALU.add)
                    else:
                        w0 = c * 8 if k < 2 else (NC - 1) * 8 - c * 8
                        o = y_v.rearrange("p j (h w) -> p j w h", h=H)[:, :, ds(w0, 8), :]
                        m = e.tensor_tensor(o, o, py3.rearrange("p j (w h) -> p j w h", w=8), ALU.add)
                    m.then_inc(yev, 1)

                g0 = e.snap(b * 24)
                delta(g0, 0, 0, 0, e.snap(g0 * 2))

                def body(k, c, par, last, nxt):
                    g = e.snap(b * 24 + (c + k * NC))
                    g16, g48 = e.snap(g * 16), e.snap(g * 48)
                    for i in range(N):
                        e.wait_ge(dbus, g16 + (2 + i + 1))
                        e.wait_ge(carry, g16 + (i + 1))
                        e.wait_ge(carry, g16 + (i + 13))
                        if i >= 2:
                            e.wait_ge(hcs, g16 + (i - 2))
                        for j in range(J):
                            e.wait_ge(da, g48 + (3 * i + j + 1))
                            e.tensor_tensor_scan(rev(hb[:, i % NH, j], k), rev(ps[:, 2 + j, 0:CH], k),
                                                 rev(dbu[:, i % 2, j], k), hst[:, i, j:j + 1],
                                                 ALU.mult, ALU.add).then_inc(scan, 1)
                        if i == 1 and last:
                            e.wait_ge(ysum, g16 + 2)
                            e.wait_ge(yev, g)
                            add_y(*last)
                        if i >= 1:
                            times_c(g16, g48, i - 1)
                        if nxt and i == 13:
                            delta(g + 1, 1 - par, *nxt, g * 2 + 2)
                    times_c(g16, g48, N - 1)

                def times_c(g16, g48, i):
                    e.wait_ge(scan, g48 + (3 + 3 * i + 3))
                    e.wait_ge(c_mm, g16 + (i + 1))
                    e.wait_ge(ysum, g16 + (i + 1))
                    e.tensor_tensor(hc[:, i % 2], hb[:, i % NH], ps[:, 1:2, 0:CH].broadcast_to([128, J, CH]),
                                    ALU.mult).then_inc(hcs, 1)

                walk(e, body)
                e.wait_ge(ysum, b * 384 + 384 + 2)
                e.wait_ge(yev, b * 24 + 24)
                add_y(K - 1, NC - 1)

            def back(b):
                n0 = e.snap(b * 32)
                e.wait_ge(x_in, b * 32 + 32)
                normalise(0, nrm)
                with e.Fori(0, 3) as cc:
                    for s in range(2):
                        o = y_v[:, :, ds(cc * 2 * CH + s * CH, CH)]
                        e.wait_ge(mu_mm, b * 6 + cc * 2 + (s + 1))
                        e.tensor_tensor(o, o, ps[:, 6 + s:7 + s, 0:CH].broadcast_to([128, J, CH]),
                                        ALU.subtract).then_inc(cen, 1)
                e.wait_ge(z_ge, b * 18 + 24)
                alone(e)
                with e.Fori(0, 3) as cc:
                    for s in range(2):
                        k = e.snap(n0 + cc * 10 + (5 * s + 12))
                        o = y_v[:, :, ds(cc * 2 * CH + s * CH, CH)]
                        zz = z_v[:, :, ds(cc * 2 * CH + s * CH, CH)]
                        e.wait_ge(rsd, b * 12 + cc * 4 + (2 * s + 2))
                        e.wait_ge(cen, b * 6 + 8)
                        e.tensor_tensor(o, o, ps[:, s:s + 1, 0:CH].broadcast_to([128, J, CH]), ALU.mult).then_inc(nrm, 1)
                        e.wait_ge(nrm, k + 1)
                        for j in range(J):
                            e.tensor_scalar(o[:, j], o[:, j], ln_w[:, j:j + 1], ln_b[:, j:j + 1],
                                            ALU.mult, ALU.add).then_inc(nrm, 1)
                        e.wait_ge(nrm, k + 4)
                        e.tensor_tensor(o, o, zz, ALU.mult).then_inc(nrm, 1)
                with e.Fori(0, 3) as cc:
                    for s in range(2):
                        for h in range(CT):
                            xo = x_v[:, h, ds(cc * 2 * CH + s * CH, CH)]
                            e.wait_ge(o_mm, b * 12 + cc * 4 + (2 * s + h + 1))
                            e.tensor_tensor(xo, xo, ps[0:CP, 2 + 2 * s + h, 0:CH], ALU.add).then_inc(x1s, 1)

            def attention(b):
                e.wait_ge(x1s, b * 12 + 16)
                groupnorm(b, 1)
                e.wait_ge(kclr, b + 1)
                def conv_tile(i):
                    p, kind = divmod(i, 3)
                    e.wait_ge(qk_ev, b * 36 + (6 * i + 6 + 2))
                    conv_taps(b * 108, i, cv2, xp2[i % 3], (q_v[:, p], kz[:, 2 * p], v_v[:, p])[kind], w_dw, b_dw)

                def norms(p):
                    for c in range(NC):
                        e.wait_ge(n_mm, b * 14 + (7 * p + c + 1))
                        e.tensor_scalar(ps[:, c % 2, 0:CH], ps[:, c % 2, 0:CH], 1e-24, None, ALU.max).then_inc(n_cl, 1)
                        if c:
                            scale_q(p, c - 1)
                    scale_q(p, NC - 1)
                    e.wait_ge(k_ac, b * 2 + (p + 1))
                    e.tensor_scalar(kn[:, p], kn[:, p], 1e-12, None, ALU.max).then_inc(k_v, 1)
                    e.wait_ge(k_v, b * 4 + (2 * p + 1))
                    e.reciprocal(ksc[:, p], kn[:, p]).then_inc(k_v, 1)

                def scale_q(p, c):
                    o = q_v[:, p, c * CH:(c + 1) * CH]
                    e.wait_ge(n_ac, b * 24 + (12 * p + 2 * c + 2))
                    e.scalar_tensor_tensor(out=o, in0=o, scalar=t_q[:, p:p + 1], in1=ps[:, c % 2, 0:CH],
                                           op0=ALU.mult, op1=ALU.mult).then_inc(qn, 1)

                for p in range(PAIRS):
                    for i in range(3 * p, 3 * p + 3):
                        conv_tile(i)
                    e.wait_ge(cv2, b * 108 + (54 * p + 54))
                    norms(p)
                for p in range(PAIRS):
                    e.wait_ge(r_mm, b * 12 + (p + 1))
                    e.reciprocal(kn[:, p], ps[:, p, 0:2 * MT]).then_inc(r_v, 1)
                    e.wait_ge(r_v, b * 4 + (2 * p + 1))
                    e.tensor_copy(spread[:, p].rearrange("p m (h c) -> p (m h) c", h=2),
                                  kn[:, p].rearrange("p (m c) -> p m c", c=1).broadcast_to([128, 2 * MT, 64]))\
                        .then_inc(r_v, 1)
                for p in range(PAIRS):
                    for g in range(5):
                        q = 5 * p + g
                        n = (min(4 * g + 4, MT) - 4 * g) * 128
                        o = q_v[:, p, g * 512:g * 512 + n]
                        e.wait_ge(r_mm, b * 12 + (q + 3))
                        e.tensor_tensor(o, o, ps[:, 2 + q % 2, 0:n], ALU.mult).then_inc(on, 1)
                with e.Fori(0, 3) as cc:
                    for s in range(2):
                        for h in range(CT):
                            xo = x_v[:, h, ds(cc * 2 * CH + s * CH, CH)]
                            e.wait_ge(p_mm, b * 12 + cc * 4 + (2 * s + h + 1))
                            e.scalar_tensor_tensor(out=xo, in0=ps[0:CP, 2 + 2 * s + h, 0:CH], scalar=b_pr[:, h:h + 1],
                                                   in1=xo, op0=ALU.add, op1=ALU.add).then_inc(x2s, 1)

            with e.Fori(0, NB) as b:
                for i, f in enumerate((front, scan_phase, back, attention)):
                    f(b)
                    barrier(e, b, i)
                wait_stored(e, b)

        @block.scalar
        def _(e):
            e.wait_ge(consts, 16 * len(loads))
            e.activation(a_neg[:], a_neg[:], ACT.Exp).then_inc(exp_a, 1)
            for s, v in ((in_ev, 2), (z_ge, 6), (qk_ev, 2), (ex, 3), (o_ev, 1)):
                e.sem_inc(s, v)
            e.wait_ge(prepared, 8)

            def group_std(b, q):
                e.wait_ge(gn_p, b * 4 + (2 * q + 2))
                e.activation(gstd[:], ps[0:CP, 7, 8:8 + CT], ACT.Sqrt, bias=eps5[0:CP]).then_inc(gn_a, 1)

            def front(b):
                group_std(b, 0)
                for j in range(J):
                    with e.Fori(0, 3) as cc:
                        for s in range(2):
                            e.wait_ge(in_mm, b * 18 + cc * 2 + (6 * j + s + 1))
                            e.activation(xpad[:, j, ds(cc * 16 + (8 * s + 1), 8), 1:1 + W],
                                         ps[:, 4 + s, 0:CH].rearrange("p (h w) -> p h w", w=W),
                                         ACT.Copy).then_inc(in_ev, 1)
                for j in range(J):
                    e.wait_ge(conv, b * 54 + (18 * j + 18))
                    e.activation(u_v[:, 0, j], u_v[:, 0, j], ACT.Gelu).then_inc(gel, 1)
                    e.wait_ge(gel, b * 6 + (2 * j + 1))
                    e.activation(u_v[:, 1, j].rearrange("p (w h) -> p w h", w=W),
                                 u_v[:, 0, j].rearrange("p (h w) -> p w h", h=H), ACT.Copy).then_inc(gel, 1)
                with e.Fori(0, 3) as cc:
                    for s in range(2):
                        for o in range(2):
                            q = 2 * s + o
                            at = cc * 2 * CH + s * CH
                            e.wait_ge(xp_mm, b * 12 + cc * 4 + (q + 1))
                            e.activation(dts[64 - 64 * o:128 - 64 * o, ds(at, CH)], ps[64:128, q, 0:CH],
                                         ACT.Copy).then_inc(xp_ev, 1)
                            for a in range(2):
                                e.activation(bc[64:96, o + 2 * a, ds(at, CH)], ps[32 * a:32 * a + 32, q, 0:CH],
                                             ACT.Copy).then_inc(xp_ev, 1)

            def scan_phase(b):
                def softplus(g, par, k, op, j):
                    x, y = dlt[:, par, j], du[:, par, j]
                    if op == "x":
                        e.wait_ge(dp_mm, g * 3 + (j + 1))
                        e.activation(x, ps[:, 0, 0:CH], ACT.Identity, bias=b_dt[:, j, k:k + 1]).then_inc(dp_rd, 1)
                    elif op == "abs":
                        e.wait_ge(dp_rd, g * 3 + (j + 1))
                        e.activation(y, x, ACT.Abs).then_inc(dp_a, 1)
                    elif op == "exp":
                        e.wait_ge(dp_a, g * 9 + (j + 1))
                        e.activation(y, y, ACT.Exp, scale=-1.0).then_inc(dp_a, 1)
                    else:
                        e.wait_ge(dp_a, g * 9 + (j + 4))
                        e.activation(y, y, ACT.Ln, bias=1.0).then_inc(dp_a, 1)

                when = {3: (("x", 0),), 4: (("abs", 0),), 5: (("x", 1),), 6: (("abs", 1),), 7: (("x", 2),),
                        8: (("abs", 2),), 9: (("exp", 0), ("exp", 1)), 10: (("exp", 2),),
                        11: (("ln", 0), ("ln", 1)), 12: (("ln", 2),)}

                def b_copy(g16, n):
                    e.wait_ge(b_mm, g16 + (n + 1))
                    e.wait_ge(dbus, g16 + (n + 1))
                    e.activation(bs[:, n % 2], ps[:, 0, 0:CH], ACT.Copy).then_inc(b_sb, 1)

                alone(e)
                e.preload_act_table_set("natural_log_exp_and_others")
                g0 = e.snap(b * 24)
                for i in when:
                    for op, j in when[i]:
                        softplus(g0, 0, 0, op, j)
                g016 = e.snap(b * 384)
                b_copy(g016, 0)
                b_copy(g016, 1)

                def body(k, c, par, last, nxt):
                    g = e.snap(b * 24 + (c + k * NC))
                    g16, g48 = e.snap(g * 16), e.snap(g * 48)
                    e.wait_ge(dp_v, g * 2 + 1)
                    for i in range(N):
                        for j in range(J):
                            e.wait_ge(scan, g48 + (3 * i + j + 1))
                            e.activation(ps[:, 2 + j, 0:CH], dlt[:, par, j], ACT.Exp,
                                         scale=a_neg[:, j, k, i:i + 1]).then_inc(da, 1)
                        if nxt and i == 4:
                            e.wait_ge(dbus, g16 + 2)
                        if nxt:
                            for op, j in when.get(i, ()):
                                softplus(g + 1, 1 - par, nxt[0], op, j)
                        if i < N - 2 or nxt:
                            b_copy(g16, i + 2)

                walk(e, body)

            def back(b):
                with e.Fori(0, 3) as cc:
                    for s in range(2):
                        for j in range(J):
                            e.wait_ge(z_mm, b * 18 + cc * 6 + (3 * s + j + 1))
                            e.activation(z_v[:, j, ds(cc * 2 * CH + s * CH, CH)], ps[:, 3 * s + j, 0:CH],
                                         ACT.Gelu).then_inc(z_ge, 1)
                with e.Fori(0, 3) as cc:
                    for s in range(2):
                        e.wait_ge(cen, b * 6 + cc * 2 + (s + 3))
                        e.activation(sq_v[:, :, ds(cc * 2 * CH + s * CH, CH)], y_v[:, :, ds(cc * 2 * CH + s * CH, CH)],
                                     ACT.Square).then_inc(sqs, 1)
                with e.Fori(0, 3) as cc:
                    for s in range(2):
                        e.wait_ge(var_mm, b * 6 + cc * 2 + (s + 1))
                        e.activation(ps[:, s, 0:CH], ps[:, s, 0:CH], ACT.Ln, bias=eps5[:]).then_inc(rsd, 1)
                        e.wait_ge(rsd, b * 12 + cc * 4 + (2 * s + 1))
                        e.activation(ps[:, s, 0:CH], ps[:, s, 0:CH], ACT.Exp, scale=-0.5).then_inc(rsd, 1)

            def attention(b):
                group_std(b, 1)
                for i in range(QT):
                    if i >= 3:
                        e.wait_ge(cv2, b * 108 + 18 * (i - 2))
                    alone(e)
                    with e.Fori(0, 3) as cc:
                        for s in range(2):
                            e.wait_ge(qk_mm, b * 36 + cc * 2 + (6 * i + s + 1))
                            e.activation(xp2[i % 3][:, ds(cc * 16 + (8 * s + 1), 8), 1:1 + W],
                                         ps[:, 6 + s, 0:CH].rearrange("p (h w) -> p h w", w=W),
                                         ACT.Identity, bias=b_qkv[:, i:i + 1]).then_inc(qk_ev, 1)
                for p in range(PAIRS):
                    e.wait_ge(cv2, b * 108 + (54 * p + 18))
                    e.activation(sqq[p], q_v[:, p], ACT.Square).then_inc(qsq, 1)
                    e.wait_ge(cv2, b * 108 + (54 * p + 36))
                    e.activation(sqk[p], kz[:, 2 * p], ACT.Square).then_inc(qsq, 1)
                    for g in range(5):
                        n = (min(4 * g + 4, MT) - 4 * g) * 128
                        e.wait_ge(vt_mm, b * 10 + (5 * p + g + 1))
                        e.activation(vt[:, 4 * g:min(4 * g + 4, MT), p],
                                     ps[:, 3 + g % 2, 0:n].rearrange("p (m c) -> p m c", c=128),
                                     ACT.Copy).then_inc(vt_ev, 1)
                    for c in range(NC):
                        r = ps[:, c % 2, 0:CH]
                        e.wait_ge(n_cl, b * 12 + (6 * p + c + 1))
                        e.activation(r, r, ACT.Ln, scale=65536.0).then_inc(n_ac, 1)
                        e.wait_ge(n_ac, b * 24 + (12 * p + 2 * c + 1))
                        e.activation(r, r, ACT.Exp, scale=-0.5, bias=ln_shift[:]).then_inc(n_ac, 1)
                    e.wait_ge(n_mm, b * 14 + (7 * p + 7))
                    e.activation(kn[:, p], ps[:, 2, 0:2 * MT], ACT.Sqrt).then_inc(k_ac, 1)
                    e.wait_ge(k_v, b * 4 + (2 * p + 2))
                    alone(e)
                    with e.Fori(0, 3) as c:
                        turn = e.snap(b * 6 + c + 3 * p)
                        base = e.snap(turn * 36)
                        for w in range(2 * MT):
                            m, h = divmod(w, 2)
                            e.wait_ge(s_mm, base + (w + 1))
                            e.wait_ge(pv, base + (w + 1))
                            e.activation(pb[:, w % 4].rearrange("p (s l) -> p s l", s=2),
                                         ps[:, 2 * (w % 3):2 * (w % 3) + 2, 0:CH], ACT.Exp,
                                         scale=ksc[:, p, w:w + 1], bias=t_neg[:, 2 * p + h:2 * p + h + 1]).then_inc(ex, 1)
                        e.wait_ge(pv, base + (2 * MT + 4))
                        e.activation(q_v[:, p, ds(c * QC, QC)].rearrange("p (s l) -> p s l", s=2),
                                     ps[:, 6:8, 0:CH], ACT.Copy).then_inc(o_ev, 1)

            with e.Fori(0, NB) as b:
                for i, f in enumerate((front, scan_phase, back, attention)):
                    f(b)
                    barrier(e, b, i)
                wait_stored(e, b)

        @block.gpsimd
        def _(e):
            e.memset(hst[:], 0.0).then_inc(carry, 16)
            for s, v in ((dbus, 2), (ysum, 2), (pv, 4)):
                e.sem_inc(s, v)
            e.wait_ge(prepared, 8)

            def clear_border(v):
                e.memset(v[..., 0:1, :], 0.0)
                e.memset(v[..., HP - 1:HP, :], 0.0)
                e.memset(v[..., 1:HP - 1, 0:1], 0.0)
                return e.memset(v[..., 1:HP - 1, HP - 1:HP], 0.0)

            def front(b):
                clear_border(xpad).then_inc(pad0, 1)

            def scan_phase(b):
                g0 = e.snap(b * 24)
                g016 = e.snap(b * 384)
                e.wait_ge(dp_v, g0 * 2 + 2)
                for q in range(2):
                    e.wait_ge(b_sb, g016 + (q + 1))
                    e.tensor_tensor(dbu[:, q % 2], du[:, 0], bs[:, q % 2:q % 2 + 1].broadcast_to([128, J, CH]),
                                    ALU.mult).then_inc(dbus, 1)

                def body(k, c, par, last, nxt):
                    g = e.snap(b * 24 + (c + k * NC))
                    g16, g48 = e.snap(g * 16), e.snap(g * 48)
                    for i in range(N):
                        e.wait_ge(scan, g48 + (3 * i + 6))
                        if isinstance(c, int) and c == NC - 1:
                            alone(e)
                            e.memset(hst[:, i], 0.0).then_inc(carry, 1)
                        else:
                            e.tensor_tensor(hst[:, i], hb[:, i % NH, :, CH - 1 if k < 2 else 0], ones[:].broadcast_to([128, J]),
                                            ALU.mult).then_inc(carry, 1)
                        if i < N - 2 or nxt:
                            if i == N - 2:
                                e.wait_ge(dp_v, g * 2 + 4)
                            e.wait_ge(b_sb, g16 + (i + 3))
                            e.tensor_tensor(dbu[:, i % 2], du[:, par if i < N - 2 else 1 - par],
                                            bs[:, i % 2:i % 2 + 1].broadcast_to([128, J, CH]), ALU.mult).then_inc(dbus, 1)

                walk(e, body)

            def back(b):
                pass

            def attention(b):
                alone(e)
                for v in xp2:
                    clear_border(v)
                for p in range(PAIRS):
                    m = e.memset(kz[0:64, 2 * p + 1], 0.0)
                m.then_inc(kclr, 1)
                for p in range(PAIRS):
                    e.wait_ge(cv2, b * 108 + (54 * p + 36))
                    e.tensor_tensor(kz[64:128, 2 * p + 1], kz[64:128, 2 * p], ones[64:128, :].broadcast_to([64, L]),
                                    ALU.mult).then_inc(kzs, 1)
                    e.wait_ge(kzs, b * 4 + (2 * p + 1))
                    e.wait_ge(qsq, b * 4 + (2 * p + 2))
                    alone(e)
                    e.memset(kz[64:128, 2 * p], 0.0).then_inc(kzs, 1)

            with e.Fori(0, NB) as b:
                for i, f in enumerate((front, scan_phase, back, attention)):
                    f(b)
                    barrier(e, b, i)
                wait_stored(e, b)

    return nc


def layouts(i):
    f = np.float32

    def col(a):
        return np.ascontiguousarray(np.moveaxis(a.reshape(J, 128, *a.shape[1:]), 0, 1))

    def heads(a, fill=0.0):
        o = np.full((QT * 128,) + a.shape[1:], fill, f)
        for s in range(3):
            for h in range(HEADS):
                at = ((h // 2) * 3 + s) * 128 + 64 * (h % 2)
                o[at:at + HD] = a[s * C + h * HD:s * C + (h + 1) * HD]
        return o

    xp = i["L0_conv_x_proj_w"]
    w_xp = np.zeros((2, 128, DI), f)
    w_dt = np.zeros((K, 128, DI), f)
    for k in range(K):
        a = k // 2
        w_xp[k % 2, 32 * a:32 * a + 2 * N] = xp[k, R:]
        w_xp[k % 2, 64 + 32 * a:64 + 32 * a + R] = xp[k, :R]
        w_dt[k, DT0[k]:DT0[k] + R] = i["L0_conv_dt_w"][k].T
    sel = np.zeros((3, 2 * N, 2 * N, 128), f)
    for n in range(2 * N):
        sel[:, n, n] = 1.0
    b_dw = heads(i["L1_conv_b_dw"])
    for p in range(PAIRS):
        for h in range(2):
            b_dw[(3 * p + 2) * 128 + 64 * h + HD] = 1.0
    w_pr = np.zeros((PAIRS, 128, C), f)
    t_q = np.ones((128, PAIRS), f)
    temp = i["L1_conv_temperature"].reshape(HEADS)
    hones, hind, ssel = np.zeros((128, 128), f), np.zeros((128, 2), f), np.zeros((128, 2), f)
    for h in range(HEADS):
        p, a = h // 2, 64 * (h % 2)
        w_pr[p, a:a + HD] = i["L1_conv_w_proj"].T[h * HD:(h + 1) * HD]
        t_q[a:a + 64, p] = temp[h]
        hones[a:a + 64, a:a + 64] = 1.0
        hind[a:a + 64, h % 2] = 1.0
        ssel[a + HD, h % 2] = 1.0
    qkv = heads(i["L1_conv_w_qkv"])
    return {
        "x": i["x"].reshape(NB, C, L),
        "w_in": np.moveaxis(i["L0_conv_in_proj_w"].T.reshape(CT, CP, 2 * DI), 0, 1),
        "w_xp": col(np.moveaxis(w_xp, 2, 0)),
        "w_dt": np.moveaxis(w_dt, 0, 1), "ident": np.eye(128, dtype=f),
        "a_logs": np.transpose(i["L0_conv_A_logs"].reshape(K, J, 128, N), (2, 1, 0, 3)),
        "ds": np.transpose(i["L0_conv_Ds"].reshape(K, J, 128), (2, 1, 0)),
        "w_cv": col(i["L0_conv_conv_w"].reshape(DI, 9)), "b_cv": col(i["L0_conv_conv_b"]),
        "b_dt": col(i["L0_conv_dt_b"].T), "ln_w": col(i["L0_conv_ln_w"]), "ln_b": col(i["L0_conv_ln_b"]),
        "w_out": col(i["L0_conv_out_proj_w"].T),
        "gmat": np.kron(np.eye(16, dtype=f), np.full((6, 6), 1.0 / 6, f)), "mean_m": np.full((128, 128), 1.0 / DI, f),
        "w_qkv": np.moveaxis(qkv.T.reshape(CT, CP, QT * 128), 0, 1),
        "b_qkv": heads(i["L1_conv_b_qkv"]).reshape(QT, 128).T,
        "w_dw": np.moveaxis(heads(i["L1_conv_w_dw"].reshape(3 * C, 9)).reshape(QT, 128, 9), 0, 1),
        "b_dw": b_dw.reshape(QT, 128).T, "w_pr": np.moveaxis(w_pr, 0, 1),
        "b_pr": i["L1_conv_b_proj"].reshape(CT, CP).T, "t_q": t_q,
        "t_all": np.broadcast_to(temp, (128, HEADS)), "hones": hones, "hind": hind, "ssel": ssel,
        "sel": sel.reshape(96, 2 * N * 128),
    }


def kernel(**inputs):
    import concourse.bacc as _bacc
    from concourse.bass_utils import run_bass_kernel_spmd as _run

    nc = _bacc.Bacc("TRN2", target_bir_lowering=False, num_devices=1)
    arrays, t = {}, {}
    for name, a in layouts({k: np.asarray(v) for k, v in inputs.items()}).items():
        a = np.ascontiguousarray(a)
        arrays[f"in_{name}"] = a
        t[name] = nc.dram_tensor(f"in_{name}", a.shape, F32, kind="ExternalInput").ap()
    out = nc.dram_tensor("out", (NB, C, L), F32, kind="ExternalOutput").ap()
    build(nc, t, out)
    r = _run(nc, [arrays], core_ids=[0])
    return r.results[0]["out"].reshape(NB, C, H, W)
```

```python
from contextlib import ExitStack

import numpy as np
import concourse.bass as bass
from concourse import mybir

F32 = mybir.dt.float32
BF16 = mybir.dt.bfloat16
ALU = mybir.AluOpType
ACT = mybir.ActivationFunctionType
ds = bass.ds

NB, C, H, W = 8, 192, 48, 48
L = H * W
CP = 96
CT = C // CP
DI = 384
J = DI // 128
K, N, R = 4, 16, 12
CH = 8 * W
NC = L // CH
HP = H + 2
PAD = HP * HP
JC = J * CH
HEADS, HD = 4, 48
PAIRS = HEADS // 2
MT = L // 128
QC = 2 * CH
QT = 6
GN_OPS = 21
LN65536 = 16.0 * float(np.log(2.0))

U = 0
DTS = U + 2 * J * L
DT0 = (64, 0, 96, 32)
BC = DTS + L
Y = BC + K * L // 2
XS = Y + J * L
NH = 4
DEL, DU, HC, DBU, HB = (XS + i * JC for i in (0, 2, 4, 6, 10))
BS = HB + NH * JC
SCAN_END = BS + 2 * CH
RES = Y
Z = J * L
SQ = 0
XN0 = Y + J * L
PADS = PAD + 4
V = 0
XP2 = V + PAIRS * L
XN1 = XP2 + 3 * PADS
AREA = SCAN_END
X = AREA - CT * L
VT = X - MT * PAIRS * 128
KZ = VT - HEADS * L
Q = KZ - PAIRS * L
PB = Q - 4 * QC
XPAD = J * L
XF = XPAD + PADS + 8
WCUR = XF + CT * L
assert XN0 + CT * L <= X and XN1 + CT * L <= Q and WCUR + CT * 128 <= PB and RES + 8 * CH <= SCAN_END
assert XF >= XPAD + L and XPAD == XP2 + L


def build(nc, t, out):
    ctx = ExitStack()
    with ctx:
        def sb(name, shape, dt=F32):
            return ctx.enter_context(nc.sbuf_tensor(name, shape, dt))

        def sem(name):
            return ctx.enter_context(nc.semaphore(name))

        w_in = sb("w_in", [CP, CT, 2 * DI])
        w_xp = sb("w_xp", [128, J, 2, 128])
        w_dt = sb("w_dt", [128, K, DI])
        ident = sb("ident", [128, 128])
        sel = sb("sel", [96, 2 * N], BF16)
        a_neg = sb("a_neg", [128, J, K, N])
        d_skip = sb("d_skip", [128, J, K])
        d_sum = sb("d_sum", [128, J, 2])
        d_diag = sb("d_diag", [128, J, 128])
        w_cv = sb("w_cv", [128, J, 9])
        b_cv = sb("b_cv", [128, J])
        b_dt = sb("b_dt", [128, J, K])
        ln_w = sb("ln_w", [128, J])
        ln_b = sb("ln_b", [128, J])
        w_out = sb("w_out", [128, J, C])
        gmat = sb("gmat", [CP, CP])
        mean_m = sb("mean_m", [128, 128])
        w_qkv = sb("w_qkv", [CP, CT, QT * 128])
        b_qkv = sb("b_qkv", [128, QT])
        w_dw = sb("w_dw", [128, QT, 9])
        b_dw = sb("b_dw", [128, QT])
        w_pr = sb("w_pr", [128, PAIRS, C])
        b_pr = sb("b_pr", [CP, CT])
        t_q = sb("t_q", [128, PAIRS])
        t_all = sb("t_all", [128, HEADS])
        t_neg = sb("t_neg", [128, HEADS])
        hones = sb("hones", [128, 128])
        hind = sb("hind", [128, 2])
        ssel = sb("ssel", [128, 2])
        eps5 = sb("eps5", [128, 1])
        ntiny = sb("ntiny", [128, 1])
        stiny = sb("stiny", [128, 1])
        ones = sb("ones", [128, 1])
        ln_shift = sb("ln_shift", [128, 1])
        hst = sb("hst", [128, N, J])
        gst = sb("gst", [CP, CT, 6, 6])
        gmv = sb("gmv", [CP, CT, 2])
        gdm = sb("gdm", [CP, CT])
        gd2 = sb("gd2", [CP, CT])
        gq = sb("gq", [CP, CT])
        gmean = sb("gmean", [CP, CT])
        glog = sb("glog", [CP, CT])
        grs = sb("grs", [CP, 2, CT])
        gnb = sb("gnb", [CP, 2, CT])
        kr = sb("kr", [128, 2 * MT])
        kn = sb("kn", [128, PAIRS, 2 * MT])
        ksc = sb("ksc", [128, PAIRS, 2 * MT])
        area = sb("area", [128, AREA])
        ps = ctx.enter_context(nc.psum_tensor("ps", [128, 8, 512], F32))

        def ar(off, n, p0=0, p1=128):
            return area[p0:p1, off:off + n]

        u_v = ar(U, 2 * J * L).rearrange("p (o j l) -> p o j l", o=2, j=J)
        dts = ar(DTS, L)
        bc = area[0:96, BC:BC + K * L // 2].bitcast(BF16).rearrange("p (k l) -> p k l", k=K)
        y_v = ar(Y, J * L).rearrange("p (j l) -> p j l", j=J)
        dlt = ar(DEL, 2 * JC).rearrange("p (b j l) -> p b j l", b=2, j=J)
        du = ar(DU, 2 * JC).rearrange("p (b j l) -> p b j l", b=2, j=J)
        dbu = ar(DBU, NH * JC).rearrange("p (b j l) -> p b j l", b=NH, j=J)
        hb = ar(HB, NH * JC).rearrange("p (b j l) -> p b j l", b=NH, j=J)
        hc = ar(HC, 2 * JC).rearrange("p (b j l) -> p b j l", b=2, j=J)
        bs = ar(BS, 2 * CH).rearrange("p (b l) -> p b l", b=2)
        xpad = ar(XPAD, PAD).rearrange("p (h w) -> p h w", h=HP)
        xf = ar(XF, CT * L, 0, CP).rearrange("p (t l) -> p t l", t=CT)
        w_cur = ar(WCUR, CT * 128, 0, CP).rearrange("p (t m) -> p t m", t=CT)
        x_v = ar(X, CT * L, 0, CP).rearrange("p (t l) -> p t l", t=CT)
        xn0 = ar(XN0, CT * L, 0, CP).rearrange("p (t l) -> p t l", t=CT)
        xn1 = ar(XN1, CT * L, 0, CP).rearrange("p (t l) -> p t l", t=CT)
        res = ar(RES, 8 * CH).rearrange("p (q a l) -> p q a l", q=4, a=2)
        z_v = ar(Z, J * L).rearrange("p (j l) -> p j l", j=J)
        sq_v = ar(SQ, J * L).rearrange("p (j l) -> p j l", j=J)
        q_v = ar(Q, PAIRS * L).rearrange("p (i l) -> p i l", i=PAIRS)
        kz = ar(KZ, HEADS * L).rearrange("p (i l) -> p i l", i=HEADS)
        v_v = ar(V, PAIRS * L).rearrange("p (i l) -> p i l", i=PAIRS)
        vt = ar(VT, PAIRS * MT * 128).rearrange("p (i m c) -> p i m c", i=PAIRS, m=MT)
        xp2 = [ar(XP2 + i * PADS, PAD).rearrange("p (h w) -> p h w", h=HP) for i in range(3)]
        pb = ar(PB, 4 * QC).rearrange("p (b l) -> p b l", b=4)
        sqq = [ar(VT + L, L), ar(XP2, L)]
        sqk = [ar(V, L), ar(XP2 + L, L)]
        spread = ar(KZ, PAIRS * L).rearrange("p (i m c) -> p i m c", i=PAIRS, m=MT)

        consts = sem("consts")
        prepared = sem("prepared")
        exp_a = sem("exp_a")
        phase = sem("phase")
        passed = sem("passed")
        x_in = sem("x_in")
        stored = sem("stored")
        gn_v = sem("gn_v")
        gn_p = sem("gn_p")
        gn_a = sem("gn_a")
        w_st = sem("w_st")
        in_mm = sem("in_mm")
        in_ev = sem("in_ev")
        pad0 = sem("pad0")
        conv = sem("conv")
        gel = sem("gel")
        uwh = sem("uwh")
        xp_mm = sem("xp_mm")
        xp_ev = sem("xp_ev")
        xp_sp = sem("xp_sp")
        b_mm = sem("b_mm")
        b_sb = sem("b_sb")
        c_mm = sem("c_mm")
        da = sem("da")
        scan = sem("scan")
        dbus = sem("dbus")
        carry = sem("carry")
        hcs = sem("hcs")
        ysum = sem("ysum")
        yev = sem("yev")
        dp_mm = sem("dp_mm")
        dp_rd = sem("dp_rd")
        dp_a = sem("dp_a")
        dp_v = sem("dp_v")
        dp_u = sem("dp_u")
        z_mm = sem("z_mm")
        z_ge = sem("z_ge")
        mu_mm = sem("mu_mm")
        cen = sem("cen")
        sqs = sem("sqs")
        var_mm = sem("var_mm")
        rsd = sem("rsd")
        xnz = sem("xnz")
        nrm = sem("nrm")
        gate = sem("gate")
        o_mm = sem("o_mm")
        x1s = sem("x1s")
        qk_mm = sem("qk_mm")
        qk_ev = sem("qk_ev")
        cv2 = sem("cv2")
        kclr = sem("kclr")
        qsq = sem("qsq")
        n_mm = sem("n_mm")
        n_ac = sem("n_ac")
        k_v = sem("k_v")
        k_ac = sem("k_ac")
        qn = sem("qn")
        kzs = sem("kzs")
        vt_mm = sem("vt_mm")
        vt_ev = sem("vt_ev")
        s_mm = sem("s_mm")
        ex = sem("ex")
        pv = sem("pv")
        o_ev = sem("o_ev")
        r_mm = sem("r_mm")
        r_v = sem("r_v")
        on = sem("on")
        p_mm = sem("p_mm")
        x2s = sem("x2s")

        loads = [
            (w_in[:], t["w_in"]), (w_xp[:], t["w_xp"]), (w_dt[:], t["w_dt"]),
            (ident[:], t["ident"]), (a_neg[:], t["a_logs"]), (d_skip[:], t["ds"]), (w_cv[:], t["w_cv"]),
            (b_cv[:], t["b_cv"]), (b_dt[:], t["b_dt"]), (ln_w[:], t["ln_w"]), (ln_b[:], t["ln_b"]),
            (w_out[:], t["w_out"]), (gmat[:], t["gmat"]), (mean_m[:], t["mean_m"]), (w_qkv[:], t["w_qkv"]),
            (b_qkv[:], t["b_qkv"]), (w_dw[:], t["w_dw"]), (b_dw[:], t["b_dw"]), (w_pr[:], t["w_pr"]),
            (b_pr[:], t["b_pr"]), (t_q[:], t["t_q"]), (t_all[:], t["t_all"]), (hones[:], t["hones"]),
            (hind[:], t["hind"]), (ssel[:], t["ssel"]),
            (area[0:96, 0:2 * N], t["sel"]),
        ]

        block = ctx.enter_context(nc.Block())

        def alone(e):
            e.sem_inc(passed, 1)

        def barrier(e, b, i):
            alone(e)
            e.drain().then_inc(phase, 1)
            e.wait_ge(phase, b * 16 + 4 * (i + 1))

        def wait_stored(e, b):
            e.wait_ge(stored, b * 16 + 16)

        def wait_conv(e, b, j):
            e.wait_ge(conv, b * 54 + (18 * j + 18))

        def wait_cv2(e, b, i):
            e.wait_ge(cv2, b * 108 + (18 * i + 18))

        def snap(e, v):
            return v if isinstance(v, int) else e.snap(v)

        def conv_taps(e, base, i, done, src, dst, w, bias):
            base = snap(e, base + 18 * i)
            acc = dst.rearrange("p (h w) -> p h w", h=H)
            for tap in range(9):
                dy, dx = divmod(tap, 3)
                for half in range(2):
                    r = H // 2 * half
                    a, x = acc[:, r:r + H // 2], src[:, r + dy:r + dy + H // 2, dx:dx + W]
                    if tap == 0:
                        e.tensor_scalar(a, x, w[:, i, 0:1], bias[:, i:i + 1], ALU.mult, ALU.add).then_inc(done, 1)
                    else:
                        e.wait_ge(done, base + (2 * tap - 1 + half))
                        e.scalar_tensor_tensor(out=a, in0=x, scalar=w[:, i, tap:tap + 1], in1=a,
                                               op0=ALU.mult, op1=ALU.add).then_inc(done, 1)

        def conv_qkv(e, b, i):
            p, kind = divmod(i, 3)
            e.wait_ge(qk_ev, b * 36 + (6 * i + 6 + 2))
            conv_taps(e, b * 108, i, cv2, xp2[i % 3], (v_v[:, p], q_v[:, p], kz[:, 2 * p])[kind], w_dw, b_dw)

        def copy_vt(e, b, p, g):
            n = (min(4 * g + 4, MT) - 4 * g) * 128
            e.wait_ge(vt_mm, b * 10 + (5 * p + g + 1))
            e.activation(vt[:, p, 4 * g:min(4 * g + 4, MT)],
                         ps[:, 3 + g % 2, 0:n].rearrange("p (m c) -> p m c", c=128), ACT.Copy).then_inc(vt_ev, 1)

        def column_copy(e, b, j):
            wait_conv(e, b, J - 1)
            e.wait_ge(gel, b * 3 + (j + 1))
            return u_v[:, 1, j].rearrange("p (w h) -> p w h", w=W), u_v[:, 0, j].rearrange("p (h w) -> p w h", h=H)

        def walk(e, body):
            for k in range(K):
                last, nxt = ((k - 1, NC - 1) if k else None), ((k + 1, 0) if k < K - 1 else None)
                body(k, 0, 0, last, (k, 1))
                with e.Fori(0, 2) as cc:
                    c = e.snap(2 * cc)
                    body(k, c + 1, 1, (k, c), (k, c + 2))
                    body(k, c + 2, 0, (k, c + 1), (k, c + 3))
                body(k, NC - 1, 1, (k, NC - 2), nxt)

        def pos(k, c):
            return c * CH if k < 2 else (NC - 1) * CH - c * CH

        def rev(ap, k):
            return ap if k < 2 else ap[:, ::-1]

        ps3 = ps[:, 2:5, 0:CH]

        def y_chunk(k, c):
            if k % 2 == 0:
                return y_v[:, :, ds(pos(k, c), CH)]
            return y_v.rearrange("p j (h w) -> p j w h", h=H)[:, :, ds(c * 8 if k < 2 else (NC - 1) * 8 - c * 8, 8), :]

        def y_psum(k):
            p = ps[:, 5:8, 0:CH]
            return p if k % 2 == 0 else p.rearrange("p j (w h) -> p j w h", w=8)

        @block.sync
        def _(e):
            for dst, src in loads:
                e.dma_start(dst, src).then_inc(consts, 16)
            e.dma_start(xf, t["x"][0:1].rearrange("o (t p) l -> p (o t) l", p=CP)).then_inc(x_in, 16)

            def image(b, nxt):
                e.wait_ge(phase, b * 16 + 8)
                e.dma_start(x_v, t["x"][ds(b, 1)].rearrange("o (t p) l -> p (o t) l", p=CP)).then_inc(x_in, 16)
                wait_cv2(e, b, QT - 1)
                e.dma_start(xf, t["x"][ds(nxt, 1)].rearrange("o (t p) l -> p (o t) l", p=CP)).then_inc(x_in, 16)
                e.wait_ge(x2s, b * 12 + 16)
                e.dma_start(out[ds(b, 1)].rearrange("o (t p) l -> p (o t) l", p=CP), x_v).then_inc(stored, 16)

            with e.Fori(0, NB - 1) as b:
                image(b, b + 1)
                alone(e)
            image(NB - 1, NB - 1)
            e.wait_ge(stored, (NB + 1) * 16)

        @block.tensor
        def _(e):
            e.wait_ge(consts, 16 * len(loads))
            e.wait_ge(prepared, 13)

            def group_sum(b, q, step):
                e.wait_ge(gn_v, (b * 2 + q) * GN_OPS + (14 + 4 * step))
                e.matmul(ps[0:CP, 5, 8 * step:8 * step + CT], gmat[:], (gq[:], gmv[:, :, 0])[step == 0],
                         start=True, stop=True).then_inc(gn_p, 1)

            def in_proj_tile(n):
                e.wait_ge(w_st, n + 1)
                for q in range(3):
                    for s in range(2):
                        for k in range(CT):
                            m = e.matmul(ps[:, 2 * q + s, 0:CH], w_cur[:, k], xf[:, k, (2 * q + s) * CH:(2 * q + s + 1) * CH],
                                         start=k == 0, stop=k == CT - 1)
                    m.then_inc(in_mm, 1)

            group_sum(0, 0, 0)
            group_sum(0, 0, 1)
            e.wait_ge(gn_v, GN_OPS)
            for j in range(J):
                if j:
                    e.wait_ge(in_ev, 3 * j)
                in_proj_tile(j)

            def front(b):
                for o in range(2):
                    e.wait_ge(gel if o == 0 else uwh, b * 3 + 3)
                    alone(e)
                    with e.Fori(0, 3) as cc:
                        for s in range(2):
                            e.wait_ge(xp_sp, b * 48 + cc * 8 + (24 * o + 4 * s + 2))
                            for j in range(J):
                                m = e.matmul(ps[:, 2 * o + s, 0:CH], w_xp[:, j, o],
                                             u_v[:, o, j, ds(cc * 2 * CH + s * CH, CH)], start=j == 0, stop=j == J - 1)
                            m.then_inc(xp_mm, 1)

            def scan_phase(b):
                def delta_tile(k, c, j, bank=0):
                    e.matmul(ps[:, bank, 0:CH], w_dt[:, k, j * 128:(j + 1) * 128], dts[:, ds(pos(k, c), CH)],
                             start=True, stop=True).then_inc(dp_mm, 1)

                def b_row(k, c, n):
                    e.matmul(ps[:, 0, 0:CH], sel[:, n:n + 1].broadcast_to([96, 128]), bc[:, k, ds(pos(k, c), CH)],
                             start=True, stop=True).then_inc(b_mm, 1)

                def c_row(k, c, n):
                    e.matmul(ps[:, 1, 0:CH], sel[:, N + n:N + n + 1].broadcast_to([96, 128]), bc[:, k, ds(pos(k, c), CH)],
                             start=True, stop=True).then_inc(c_mm, 1)

                c_row(0, 0, 0)
                for j in range(J):
                    delta_tile(0, 0, j, 2 + j)
                for n in range(5):
                    if n:
                        e.wait_ge(b_sb, b * 384 + n)
                    b_row(0, 0, n)

                def body(k, c, par, last, nxt):
                    g = e.snap(b * 24 + (c + k * NC))
                    g16, g3 = e.snap(g * 16), e.snap(g * 3)
                    for i in range(N):
                        e.wait_ge(hcs, g16 + (i + 2))
                        if i < N - 1 or nxt:
                            c_row(*((k, c, i + 1) if i < N - 1 else (*nxt, 0)))
                        if i < N - 5 or nxt:
                            if nxt and i in (1, 3, 5):
                                e.wait_ge(dp_rd, g3 + (4 + i // 2))
                            else:
                                e.wait_ge(b_sb, g16 + (i + 5))
                            b_row(*((k, c, i + 5) if i < N - 5 else (*nxt, i + 5 - N)))
                        if i == 0:
                            e.wait_ge(yev, g + 1)
                        for j in range(J):
                            m = e.matmul(ps[:, 5 + j, 0:CH], ident[:], hc[:, i % 2, j], start=i == 0, stop=i == N - 1)
                            if nxt and i in (0, 2, 4) and j == 0:
                                e.wait_ge(b_sb, g16 + (i + 6))
                                delta_tile(*nxt, i // 2)
                        m.then_inc(ysum, 1)
                        if i in (8, 10, 12):
                            j = (i - 8) // 2
                            if k == 0:
                                e.matmul(ps[:, 5 + j, 0:CH], d_diag[:, j], u_v[:, 0, j, ds(pos(k, c), CH)],
                                         start=False, stop=False)
                            else:
                                e.matmul(y_psum(k)[:, j], ident[:], y_chunk(k, c)[:, j], start=False, stop=False)

                walk(e, body)

            def back(b):
                alone(e)
                with e.Fori(0, 3) as cc:
                    for s in range(2):
                        e.wait_ge(cen, b * 6 + cc * 2 + (s + 1))
                        for j in range(J):
                            m = e.matmul(ps[:, 6 + s, 0:CH], mean_m[:], y_v[:, j, ds(cc * 2 * CH + s * CH, CH)],
                                         start=j == 0, stop=j == J - 1)
                        m.then_inc(mu_mm, 1)
                with e.Fori(0, 3) as cc:
                    for s in range(2):
                        e.wait_ge(sqs, b * 6 + cc * 2 + (s + 1))
                        e.wait_ge(nrm, b * 18 + cc * 6 + (3 * s + 3))
                        for j in range(J):
                            m = e.matmul(ps[:, s, 0:CH], mean_m[:], sq_v[:, j, ds(cc * 2 * CH + s * CH, CH)],
                                         start=j == 0, stop=j == J - 1)
                        m.then_inc(var_mm, 1)
                e.wait_ge(xnz, b * 2 + 2)
                e.wait_ge(cen, b * 6 + 8)
                alone(e)
                with e.Fori(0, 3) as cc:
                    for s in range(2):
                        for j in range(J):
                            e.wait_ge(z_ge, b * 18 + cc * 6 + (3 * s + j + 1))
                            for k in range(CT):
                                m = e.matmul(ps[:, 2 + 3 * s + j, 0:CH], w_in[:, k, DI + j * 128:DI + (j + 1) * 128],
                                             xn0[:, k, ds(cc * 2 * CH + s * CH, CH)], start=k == 0, stop=k == CT - 1)
                            m.then_inc(z_mm, 1)
                e.wait_ge(z_ge, b * 18 + 24)
                alone(e)
                with e.Fori(0, 3) as cc:
                    for s in range(2):
                        e.wait_ge(gate, b * 18 + cc * 6 + (3 * s + 3))
                        for h in range(CT):
                            e.wait_ge(x1s, b * 12 + cc * 4 + (2 * s + h + 1))
                            for j in range(J):
                                m = e.matmul(ps[0:CP, 2 * s + h, 0:CH], w_out[:, j, h * CP:(h + 1) * CP],
                                             y_v[:, j, ds(cc * 2 * CH + s * CH, CH)], start=j == 0, stop=j == J - 1)
                            m.then_inc(o_mm, 1)

            def attention(b):
                group_sum(b, 1, 0)
                group_sum(b, 1, 1)
                e.wait_ge(gn_v, b * 2 * GN_OPS + 2 * GN_OPS)
                alone(e)

                def qkv(i):
                    with e.Fori(0, 3) as cc:
                        for s in range(2):
                            e.wait_ge(qk_ev, b * 36 + cc * 2 + (6 * i + s + 1))
                            for k in range(CT):
                                m = e.matmul(ps[:, 6 + s, 0:CH], w_qkv[:, k, i * 128:(i + 1) * 128],
                                             xn1[:, k, ds(cc * 2 * CH + s * CH, CH)], start=k == 0, stop=k == CT - 1)
                            m.then_inc(qk_mm, 1)

                def transpose_v(p, g):
                    if g >= 2:
                        e.wait_ge(vt_ev, b * 10 + (5 * p + g - 1))
                    for m in range(4 * g, min(4 * g + 4, MT)):
                        i = e.matmul(ps[:, 3 + g % 2, (m % 4) * 128:(m % 4) * 128 + 128],
                                     v_v[:, p, m * 128:(m + 1) * 128], ident[:], start=True, stop=True)
                    i.then_inc(vt_mm, 1)

                def q_norm(p, c):
                    if c == 0:
                        e.wait_ge(qsq, b * 4 + 2 * p + 1)
                    if c >= 2:
                        e.wait_ge(n_ac, b * 36 + (18 * p + 3 * c - 3))
                    e.matmul(ps[:, c % 2, 0:CH], hones[:], sqq[p][:, c * CH:(c + 1) * CH],
                             start=True, stop=True).then_inc(n_mm, 1)

                def k_norms(p):
                    e.wait_ge(qsq, b * 4 + 2 * p + 2)
                    for m in range(MT):
                        i = e.matmul(ps[:, 2, 2 * m:2 * m + 2], sqk[p][:, m * 128:(m + 1) * 128], hind[:],
                                     start=True, stop=True)
                    i.then_inc(n_mm, 1)

                def row_sums(p):
                    e.wait_ge(o_ev, b * 6 + (3 * p + 3 + 1))
                    for m in range(MT):
                        i = e.matmul(ps[:, 6 - 5 * p, 2 * m:2 * m + 2], q_v[:, p, m * 128:(m + 1) * 128], ssel[:],
                                     start=True, stop=True)
                    i.then_inc(r_mm, 1)

                def spread_inverses(p):
                    e.wait_ge(r_v, b * 4 + (2 * p + 2))
                    for g in range(5):
                        q = 5 * p + g
                        if g >= 2:
                            e.wait_ge(on, b * 10 + (q - 1))
                        for m in range(4 * g, min(4 * g + 4, MT)):
                            i = e.matmul(ps[:, 6 - 4 * p + g % 2, (m % 4) * 128:(m % 4) * 128 + 128],
                                         spread[:, p, m], ident[:], start=True, stop=True)
                        i.then_inc(r_mm, 1)

                for p in range(PAIRS):
                    if p == 0:
                        for i in range(3):
                            qkv(i)
                        wait_cv2(e, b, 0)
                        for g in range(5):
                            transpose_v(0, g)
                        qkv(3)
                        for c in range(NC):
                            q_norm(0, c)
                        qkv(4)
                        qkv(5)
                        k_norms(0)
                        e.wait_ge(qk_ev, b * 36 + 36 + 2)
                    else:
                        e.wait_ge(ex, (b * 6 + 3) * 36 + 3)
                        group_sum(b + 1, 0, 0)
                        for c in range(NC):
                            if c == 2:
                                row_sums(0)
                                group_sum(b + 1, 0, 1)
                            if c == 4:
                                spread_inverses(0)
                            q_norm(1, c)
                        k_norms(1)
                        wait_cv2(e, b, 3)
                        for g in range(5):
                            transpose_v(1, g)
                        e.wait_ge(gn_v, (b + 1) * 2 * GN_OPS + GN_OPS)
                        e.wait_ge(on, b * 10 + 5)
                    e.wait_ge(vt_ev, b * 10 + (5 * p + 5))
                    e.wait_ge(qn, b * 2 + (p + 1))
                    e.wait_ge(kzs, b * 4 + (2 * p + 2))
                    e.wait_ge(k_ac, b * 6 + (3 * p + 3))
                    alone(e)
                    with e.Fori(0, 3) as c:
                        turn = e.snap(b * 6 + c + 3 * p)
                        base = e.snap(turn * 36)

                        def scores(w):
                            m, h = divmod(w, 2)
                            e.wait_ge(ex, base + (w + 1))
                            if p == 1 and w < 3:
                                e.wait_ge(in_ev, b * 9 + c * 3 + (3 * J + 1 + w))
                            for s in range(2):
                                i = e.matmul(ps[:, 2 * (w % 3) + s, 0:CH], kz[:, 2 * p + h, m * 128:(m + 1) * 128],
                                             q_v[:, p, ds(c * QC + s * CH, CH)], start=True, stop=True)
                            i.then_inc(s_mm, 1)

                        def values(w):
                            m, h = divmod(w, 2)
                            e.wait_ge(ex, base + (w + 4))
                            if w == 0:
                                e.wait_ge(o_ev, turn + 1)
                            for s in range(2):
                                i = e.matmul(ps[64 * h:64 * h + 64, 6 + s, 0:CH], vt[:, p, m, 64 * h:64 * h + 64],
                                             pb[:, w % 4, s * CH:(s + 1) * CH], start=m == 0, stop=m == MT - 1)
                            i.then_inc(pv, 1)

                        if p == 1:
                            e.wait_ge(ex, base + 3)
                            in_proj_tile(b * 3 + c + 3)
                        scores(0)
                        scores(1)
                        for m in range(MT):
                            for w in (2 * m + 2, 2 * m + 3):
                                if w < 2 * MT:
                                    scores(w)
                            values(2 * m)
                            values(2 * m + 1)
                row_sums(1)
                spread_inverses(1)
                for c in range(NC):
                    e.wait_ge(on, b * 10 + (5 + -(-(c + 1) * CH // 512)))
                    for h in range(CT):
                        e.wait_ge(x2s, b * 12 + (2 * c + h + 1))
                        for p in range(PAIRS):
                            m = e.matmul(ps[0:CP, 4 + 2 * (c % 2) + h, 0:CH], w_pr[:, p, h * CP:(h + 1) * CP],
                                         q_v[:, p, c * CH:(c + 1) * CH], start=p == 0, stop=p == PAIRS - 1)
                        m.then_inc(p_mm, 1)

            with e.Fori(0, NB) as b:
                for i, f in enumerate((front, scan_phase, back, attention)):
                    if i == 1:
                        wait_stored(e, b)
                        alone(e)
                    f(b)
                    barrier(e, b, i)

        @block.vector
        def _(e):
            e.memset(ones[:], 1.0).then_inc(prepared, 1)
            e.memset(eps5[:], 1e-5).then_inc(prepared, 1)
            e.memset(ntiny[:], -1e-24).then_inc(prepared, 1)
            e.memset(stiny[:], 65536e-24).then_inc(prepared, 1)
            e.memset(ln_shift[:], 0.5 * LN65536).then_inc(prepared, 1)
            e.wait_ge(consts, 16 * len(loads))
            e.tensor_copy(sel[:], area[0:96, 0:2 * N]).then_inc(prepared, 1)
            e.scalar_tensor_tensor(out=t_neg[:], in0=t_all[:], scalar=-1.0, in1=t_all[:],
                                   op0=ALU.mult, op1=ALU.min).then_inc(prepared, 1)
            e.tensor_tensor(d_sum[:], d_skip[:, :, 0:2], d_skip[:, :, 2:4], ALU.add).then_inc(prepared, 1)
            e.wait_ge(prepared, 8)
            e.tensor_tensor(d_sum[:, :, 0], d_sum[:, :, 0], d_sum[:, :, 1], ALU.add).then_inc(prepared, 1)
            e.wait_ge(prepared, 9)
            for j in range(J):
                e.tensor_scalar(d_diag[:, j], ident[:], d_sum[:, j, 0:1], None, ALU.mult).then_inc(prepared, 1)
            e.wait_ge(exp_a, 1)
            e.tensor_scalar(a_neg[:], a_neg[:], -1.0, None, ALU.mult).then_inc(prepared, 1)
            for s, v in ((xp_sp, 8), (scan, 3), (hcs, 1), (yev, 1), (cen, 2), (x1s, 4), (x2s, 4), (nrm, 6), (stored, 16)):
                e.sem_inc(s, v)
            e.wait_ge(prepared, 13)

            def channel_stats(x):
                for k in range(CT):
                    for i in range(6):
                        e.bn_stats(gst[:, k, i], x[:, k, i * CH:(i + 1) * CH]).then_inc(gn_v, 1)

            def groupnorm(b, q, x, xn, between=lambda: None):
                g = snap(e, (b * 2 + q) * GN_OPS)
                e.wait_ge(gn_v, g + 12)
                alone(e)
                for k in range(CT):
                    e.bn_aggr(gmv[:, k], gst[:, k].rearrange("p a c -> p (a c)")).then_inc(gn_v, 1)
                e.wait_ge(gn_v, g + 14)
                e.wait_ge(gn_p, b * 4 + (2 * q + 1))
                e.tensor_tensor(gdm[:], gmv[:, :, 0], ps[0:CP, 5, 0:CT], ALU.subtract).then_inc(gn_v, 1)
                e.tensor_copy(gmean[:], ps[0:CP, 5, 0:CT]).then_inc(gn_v, 1)
                e.wait_ge(gn_v, g + 16)
                e.tensor_tensor(gd2[:], gdm[:], gdm[:], ALU.mult).then_inc(gn_v, 1)
                e.wait_ge(gn_v, g + 17)
                e.tensor_tensor(gq[:], gd2[:], gmv[:, :, 1], ALU.add).then_inc(gn_v, 1)
                between()
                e.wait_ge(gn_a, b * 4 + (2 * q + 2))
                e.scalar_tensor_tensor(out=gnb[:, q], in0=gmean[:], scalar=-1.0, in1=grs[:, q],
                                       op0=ALU.mult, op1=ALU.mult).then_inc(gn_v, 1)
                e.wait_ge(gn_v, g + 19)
                for k in range(CT):
                    e.tensor_scalar(xn[:, k], x[:, k], grs[:, q, k:k + 1], gnb[:, q, k:k + 1],
                                    ALU.mult, ALU.add).then_inc(gn_v, 1)

            def conv_tiles(b):
                e.wait_ge(pad0, b + 1)
                for j in range(J):
                    e.wait_ge(in_ev, b * 9 + (3 * j + 3))
                    conv_taps(e, b * 54, j, conv, xpad, u_v[:, 0, j], w_cv, b_cv)

            e.wait_ge(x_in, 16)
            channel_stats(xf)
            groupnorm(0, 0, xf, xf)
            conv_tiles(0)

            def front(b):
                o, u = column_copy(e, b, 0)
                e.tensor_copy(o, u).then_inc(uwh, 1)
                for o in range(2):
                    alone(e)
                    with e.Fori(0, 3) as cc:
                        for s in range(2):
                            q = 2 * o + s
                            done = e.snap(b * 48 + cc * 8 + (24 * o + 4 * s + 8))
                            part = bc[:, o:K:2, ds(cc * 2 * CH + s * CH, CH)]
                            for a in range(2):
                                e.wait_ge(xp_ev, b * 36 + cc * 6 + (18 * o + 3 * s + 2 + a))
                                e.tensor_tensor(res[0:32, q, a], ps[32 * a:32 * a + 32, q, 0:CH], part[64:96, a],
                                                ALU.subtract).then_inc(xp_sp, 1)
                            e.wait_ge(xp_sp, done + 2)
                            e.tensor_copy(part[0:32], res[0:32, q]).then_inc(xp_sp, 1)
                            e.wait_ge(xp_sp, done + 3)
                            e.tensor_tensor(part[32:64], res[0:32, q], part[0:32], ALU.subtract).then_inc(xp_sp, 1)

            def scan_phase(b):
                def delta(g, par):
                    e.wait_ge(dp_a, g * 9 + 9)
                    e.scalar_tensor_tensor(out=dlt[:, par], in0=dlt[:, par], scalar=0.0, in1=du[:, par],
                                           op0=ALU.max, op1=ALU.add).then_inc(dp_v, 1)

                delta(e.snap(b * 24), 0)

                def body(k, c, par, last, nxt):
                    g = e.snap(b * 24 + (c + k * NC))
                    g16, g48 = e.snap(g * 16), e.snap(g * 48)
                    for i in range(N):
                        e.wait_ge(dbus, g16 + (2 + i + 1))
                        e.wait_ge(carry, g16 + (i + 1))
                        e.wait_ge(carry, g16 + (i + 13))
                        if i >= 2:
                            e.wait_ge(hcs, g16 + (i - 2))
                        for j in range(J):
                            e.wait_ge(da, g48 + (3 * i + j + 1))
                            e.tensor_tensor_scan(rev(hb[:, i % NH, j], k), rev(ps[:, 2 + j, 0:CH], k),
                                                 rev(dbu[:, i % NH, j], k), hst[:, i, j:j + 1],
                                                 ALU.mult, ALU.add).then_inc(scan, 1)
                        if i >= 1 or last:
                            times_c(g16, g48, i - 1)
                        if nxt and i == 11:
                            delta(g + 1, 1 - par)

                def times_c(g16, g48, i):
                    e.wait_ge(scan, g48 + (3 + 3 * i + 3))
                    e.wait_ge(c_mm, g16 + (i + 1))
                    e.wait_ge(ysum, g16 + (i + 1))
                    e.tensor_tensor(hc[:, i % 2], hb[:, i % NH], ps[:, 1:2, 0:CH].broadcast_to([128, J, CH]),
                                    ALU.mult).then_inc(hcs, 1)

                walk(e, body)
                times_c(e.snap(b * 384 + 384), e.snap(b * 1152 + 1152), -1)

            def back(b):
                alone(e)
                with e.Fori(0, 3) as cc:
                    for s in range(2):
                        o = y_v[:, :, ds(cc * 2 * CH + s * CH, CH)]
                        e.wait_ge(mu_mm, b * 6 + cc * 2 + (s + 1))
                        e.tensor_tensor(o, o, ps[:, 6 + s:7 + s, 0:CH].broadcast_to([128, J, CH]),
                                        ALU.subtract).then_inc(cen, 1)
                e.wait_ge(cen, b * 6 + 8)
                alone(e)
                with e.Fori(0, 3) as cc:
                    for s in range(2):
                        e.wait_ge(rsd, b * 12 + cc * 4 + (2 * s + 2))
                        for j in range(J):
                            o = y_v[:, j, ds(cc * 2 * CH + s * CH, CH)]
                            e.scalar_tensor_tensor(out=o, in0=o, scalar=ln_w[:, j:j + 1], in1=ps[:, s, 0:CH],
                                                   op0=ALU.mult, op1=ALU.mult).then_inc(nrm, 1)
                e.wait_ge(nrm, b * 18 + 24)
                alone(e)
                with e.Fori(0, 3) as cc:
                    for s in range(2):
                        for j in range(J):
                            o = y_v[:, j, ds(cc * 2 * CH + s * CH, CH)]
                            e.wait_ge(z_ge, b * 18 + cc * 6 + (3 * s + j + 7))
                            e.scalar_tensor_tensor(out=o, in0=o, scalar=ln_b[:, j:j + 1],
                                                   in1=z_v[:, j, ds(cc * 2 * CH + s * CH, CH)],
                                                   op0=ALU.add, op1=ALU.mult).then_inc(gate, 1)
                e.wait_ge(x_in, b * 32 + 32)
                alone(e)
                with e.Fori(0, 3) as cc:
                    for s in range(2):
                        for h in range(CT):
                            xo = x_v[:, h, ds(cc * 2 * CH + s * CH, CH)]
                            e.wait_ge(o_mm, b * 12 + cc * 4 + (2 * s + h + 1))
                            e.tensor_tensor(xo, xo, ps[0:CP, 2 * s + h, 0:CH], ALU.add).then_inc(x1s, 1)
                        for h in range(CT):
                            e.wait_ge(x1s, b * 12 + cc * 4 + (2 * s + h + 5))
                            e.bn_stats(gst[:, h, ds(cc * 2 + s, 1)].rearrange("p a c -> p (a c)"),
                                       x_v[:, h, ds(cc * 2 * CH + s * CH, CH)]).then_inc(gn_v, 1)

            def attention(b):
                groupnorm(b, 1, x_v, xn1)
                e.wait_ge(kclr, b + 1)

                def scale_q(p):
                    e.wait_ge(n_ac, b * 36 + (18 * p + 18))
                    wait_cv2(e, b, 3 * p + 1)
                    e.scalar_tensor_tensor(out=q_v[:, p], in0=q_v[:, p], scalar=t_q[:, p:p + 1], in1=sqq[p],
                                           op0=ALU.mult, op1=ALU.mult).then_inc(qn, 1)

                def invert_sums(p):
                    e.wait_ge(r_mm, b * 12 + (6 * p + 1))
                    e.reciprocal(kn[:, p], ps[:, 6 - 5 * p, 0:2 * MT]).then_inc(r_v, 1)
                    e.wait_ge(r_v, b * 4 + (2 * p + 1))
                    e.tensor_copy(spread[:, p].rearrange("p m (h c) -> p (m h) c", h=2),
                                  kn[:, p].rearrange("p (m c) -> p m c", c=1).broadcast_to([128, 2 * MT, 64]))\
                        .then_inc(r_v, 1)

                def divide(p):
                    for g in range(5):
                        n = (min(4 * g + 4, MT) - 4 * g) * 128
                        o = q_v[:, p, g * 512:g * 512 + n]
                        e.wait_ge(r_mm, b * 12 + (6 * p + g + 2))
                        e.tensor_tensor(o, o, ps[:, 6 - 4 * p + g % 2, 0:n], ALU.mult).then_inc(on, 1)

                def newton_k(p):
                    n = e.snap(b * 8 + 4 * p)
                    e.wait_ge(k_ac, b * 6 + (3 * p + 3))
                    e.tensor_tensor(kr[:], ksc[:, p], ksc[:, p], ALU.mult).then_inc(k_v, 1)
                    e.wait_ge(k_v, n + 1)
                    e.scalar_tensor_tensor(out=kr[:], in0=kn[:, p], scalar=1e-24, in1=kr[:],
                                           op0=ALU.add, op1=ALU.mult).then_inc(k_v, 1)
                    e.wait_ge(k_v, n + 2)
                    e.tensor_scalar(kr[:], kr[:], -0.5, 1.5, ALU.mult, ALU.add).then_inc(k_v, 1)
                    e.wait_ge(k_v, n + 3)
                    e.tensor_tensor(ksc[:, p], ksc[:, p], kr[:], ALU.mult).then_inc(k_v, 1)

                for i in range(3):
                    conv_qkv(e, b, i)
                wait_cv2(e, b, 2)
                e.wait_ge(vt_mm, b * 10 + 5)
                e.wait_ge(n_mm, b * 14 + 1)
                e.tensor_tensor(sqk[0], kz[:, 0], kz[:, 0], ALU.mult).then_inc(qsq, 1)
                scale_q(0)
                newton_k(0)
                for i in range(3, 6):
                    conv_qkv(e, b, i)
                    if i > 3:
                        wait_cv2(e, b, i)
                        a, sq = (q_v[:, 1], sqq[1]) if i == 4 else (kz[:, 2], sqk[1])
                        e.tensor_tensor(sq, a, a, ALU.mult).then_inc(qsq, 1)
                e.wait_ge(x_in, b * 32 + 48)
                channel_stats(xf)
                groupnorm(b + 1, 0, xf, xf, between=lambda: invert_sums(0))
                divide(0)
                scale_q(1)
                newton_k(1)
                e.wait_ge(n_mm, b * 14 + 14)
                conv_tiles(b + 1)
                invert_sums(1)
                divide(1)
                for c in range(NC):
                    for h in range(CT):
                        xo = x_v[:, h, c * CH:(c + 1) * CH]
                        e.wait_ge(p_mm, b * 12 + (2 * c + h + 1))
                        e.scalar_tensor_tensor(out=xo, in0=ps[0:CP, 4 + 2 * (c % 2) + h, 0:CH], scalar=b_pr[:, h:h + 1],
                                               in1=xo, op0=ALU.add, op1=ALU.add).then_inc(x2s, 1)

            with e.Fori(0, NB) as b:
                for i, f in enumerate((front, scan_phase, back, attention)):
                    if i == 1:
                        wait_stored(e, b)
                        alone(e)
                    f(b)
                    barrier(e, b, i)

        @block.scalar
        def _(e):
            e.wait_ge(consts, 16 * len(loads))
            e.activation(a_neg[:], a_neg[:], ACT.Exp).then_inc(exp_a, 1)
            for s, v in ((z_ge, 6), (qk_ev, 2), (ex, 3), (o_ev, 1)):
                e.sem_inc(s, v)
            e.wait_ge(prepared, 13)

            def group_std(b, q):
                e.wait_ge(gn_p, b * 4 + (2 * q + 2))
                e.activation(glog[:], ps[0:CP, 5, 8:8 + CT], ACT.Ln, bias=eps5[0:CP]).then_inc(gn_a, 1)
                e.wait_ge(gn_a, b * 4 + (2 * q + 1))
                e.activation(grs[:, q], glog[:], ACT.Exp, scale=-0.5).then_inc(gn_a, 1)

            def pad_tile(n):
                for q in range(3):
                    e.wait_ge(in_mm, n * 3 + (q + 1))
                    e.activation(xpad[:, 16 * q + 1:16 * q + 17, 1:1 + W].rearrange("p (a h) w -> p a h w", a=2),
                                 ps[:, 2 * q:2 * q + 2, 0:CH].rearrange("p a (h w) -> p a h w", w=W),
                                 ACT.Copy).then_inc(in_ev, 1)

            e.preload_act_table_set("natural_log_exp_and_others")
            group_std(0, 0)
            for j in range(J):
                if j:
                    wait_conv(e, 0, j - 1)
                pad_tile(j)

            def front(b):
                alone(e)
                e.preload_act_table_set("gelu_and_others")
                for j in range(J):
                    wait_conv(e, b, j)
                    e.activation(u_v[:, 0, j], u_v[:, 0, j], ACT.Gelu).then_inc(gel, 1)
                o, u = column_copy(e, b, 2)
                e.activation(o, u, ACT.Copy).then_inc(uwh, 1)
                for o in range(2):
                    with e.Fori(0, 3) as cc:
                        for s in range(2):
                            q = 2 * o + s
                            at = cc * 2 * CH + s * CH
                            e.wait_ge(xp_mm, b * 12 + cc * 2 + (6 * o + s + 1))
                            e.activation(dts[64 - 64 * o:128 - 64 * o, ds(at, CH)], ps[64:128, q, 0:CH],
                                         ACT.Copy).then_inc(xp_ev, 1)
                            for a in range(2):
                                e.activation(bc[64:96, o + 2 * a, ds(at, CH)], ps[32 * a:32 * a + 32, q, 0:CH],
                                             ACT.Copy).then_inc(xp_ev, 1)

            def scan_phase(b):
                def softplus(g, par, k, op, j, bank=0):
                    x, y = dlt[:, par, j], du[:, par, j]
                    if op == "x":
                        e.wait_ge(dp_mm, g * 3 + (j + 1))
                        e.activation(x, ps[:, bank, 0:CH], ACT.Identity, bias=b_dt[:, j, k:k + 1]).then_inc(dp_rd, 1)
                    elif op == "abs":
                        e.wait_ge(dp_rd, g * 3 + (j + 1))
                        e.activation(y, x, ACT.Abs).then_inc(dp_a, 1)
                    elif op == "exp":
                        e.wait_ge(dp_a, g * 9 + (j + 1))
                        e.activation(y, y, ACT.Exp, scale=-1.0).then_inc(dp_a, 1)
                    else:
                        e.wait_ge(dp_a, g * 9 + (j + 4))
                        e.activation(y, y, ACT.Ln, bias=1.0).then_inc(dp_a, 1)

                when = {3: (("x", 0),), 4: (("abs", 0),), 5: (("x", 1),), 6: (("abs", 1),), 7: (("x", 2),),
                        8: (("abs", 2), ("exp", 0)), 9: (("exp", 1), ("exp", 2)), 10: (("ln", 0), ("ln", 1)),
                        11: (("ln", 2),)}

                def b_copy(g16, n):
                    e.wait_ge(b_mm, g16 + (n + 1))
                    e.wait_ge(dbus, g16 + (n + 1))
                    e.activation(bs[:, n % 2], ps[:, 0, 0:CH], ACT.Copy).then_inc(b_sb, 1)

                def store_y(k, c, n):
                    e.wait_ge(ysum, n + 2)
                    e.activation(y_chunk(k, c), y_psum(k), ACT.Copy).then_inc(yev, 1)

                alone(e)
                e.preload_act_table_set("natural_log_exp_and_others")
                g0 = e.snap(b * 24)
                for i in when:
                    for op, j in when[i]:
                        softplus(g0, 0, 0, op, j, 2 + j)
                g016 = e.snap(b * 384)
                b_copy(g016, 0)
                b_copy(g016, 1)
                b_copy(g016, 2)

                def body(k, c, par, last, nxt):
                    g = e.snap(b * 24 + (c + k * NC))
                    g16, g48 = e.snap(g * 16), e.snap(g * 48)
                    e.wait_ge(dp_v, g + 1)
                    for i in range(N):
                        for j in range(J):
                            e.wait_ge(scan, g48 + (3 * i + j + 1))
                            e.activation(ps[:, 2 + j, 0:CH], dlt[:, par, j], ACT.Exp,
                                         scale=a_neg[:, j, k, i:i + 1]).then_inc(da, 1)
                        if i == 2 and last:
                            store_y(*last, g16)
                        if nxt and i == 4:
                            e.wait_ge(dbus, g16 + 2)
                        if nxt:
                            for op, j in when.get(i, ()):
                                softplus(g + 1, 1 - par, nxt[0], op, j)
                        if i < N - 3 or nxt:
                            b_copy(g16, i + 3)

                walk(e, body)
                store_y(K - 1, NC - 1, b * 384 + 384)

            def back(b):
                with e.Fori(0, 3) as cc:
                    for s in range(2):
                        e.wait_ge(cen, b * 6 + cc * 2 + (s + 3))
                        e.activation(sq_v[:, :, ds(cc * 2 * CH + s * CH, CH)], y_v[:, :, ds(cc * 2 * CH + s * CH, CH)],
                                     ACT.Square).then_inc(sqs, 1)
                with e.Fori(0, 3) as cc:
                    for s in range(2):
                        e.wait_ge(var_mm, b * 6 + cc * 2 + (s + 1))
                        e.activation(ps[:, s, 0:CH], ps[:, s, 0:CH], ACT.Ln, bias=eps5[:]).then_inc(rsd, 1)
                        e.wait_ge(rsd, b * 12 + cc * 4 + (2 * s + 1))
                        e.activation(ps[:, s, 0:CH], ps[:, s, 0:CH], ACT.Exp, scale=-0.5).then_inc(rsd, 1)
                e.preload_act_table_set("gelu_and_others")
                with e.Fori(0, 3) as cc:
                    for s in range(2):
                        for j in range(J):
                            e.wait_ge(z_mm, b * 18 + cc * 6 + (3 * s + j + 1))
                            e.activation(z_v[:, j, ds(cc * 2 * CH + s * CH, CH)], ps[:, 2 + 3 * s + j, 0:CH],
                                         ACT.Gelu).then_inc(z_ge, 1)
                e.preload_act_table_set("natural_log_exp_and_others")

            def attention(b):
                group_std(b, 1)

                def pad_qkv(i):
                    if i >= 3:
                        wait_cv2(e, b, i - 3)
                    alone(e)
                    with e.Fori(0, 3) as cc:
                        for s in range(2):
                            e.wait_ge(qk_mm, b * 36 + cc * 2 + (6 * i + s + 1))
                            e.activation(xp2[i % 3][:, ds(cc * 16 + (8 * s + 1), 8), 1:1 + W],
                                         ps[:, 6 + s, 0:CH].rearrange("p (h w) -> p h w", w=W),
                                         ACT.Identity, bias=b_qkv[:, i:i + 1]).then_inc(qk_ev, 1)

                def root(x, y, z, w, done, n):
                    e.activation(y, x, ACT.Relu, bias=ntiny[:]).then_inc(done, 1)
                    e.wait_ge(done, n + 1)
                    e.activation(z, y, ACT.Ln, scale=65536.0, bias=stiny[:]).then_inc(done, 1)
                    e.wait_ge(done, n + 2)
                    e.activation(w, z, ACT.Exp, scale=-0.5, bias=ln_shift[:]).then_inc(done, 1)

                def q_norm(p, c):
                    e.wait_ge(n_mm, b * 14 + (7 * p + c + 1))
                    s = ps[:, c % 2, 0:CH]
                    root(s, s, s, sqq[p][:, c * CH:(c + 1) * CH], n_ac,
                         b * 36 + (18 * p + 3 * c))

                def k_norms(p):
                    e.wait_ge(n_mm, b * 14 + (7 * p + 7))
                    root(ps[:, 2, 0:2 * MT], kn[:, p], ksc[:, p], ksc[:, p], k_ac, b * 6 + 3 * p)

                for p in range(PAIRS):
                    if p == 0:
                        for i in range(3):
                            pad_qkv(i)
                        for g in range(5):
                            copy_vt(e, b, 0, g)
                        pad_qkv(3)
                        wait_cv2(e, b, 1)
                        e.activation(sqq[0], q_v[:, 0], ACT.Square).then_inc(qsq, 1)
                        for c in range(NC):
                            q_norm(0, c)
                        pad_qkv(4)
                        pad_qkv(5)
                        k_norms(0)
                    else:
                        for c in range(NC):
                            if c == 2:
                                group_std(b + 1, 0)
                            q_norm(1, c)
                        k_norms(1)
                        for g in range(5):
                            copy_vt(e, b, 1, g)
                    e.wait_ge(k_v, b * 8 + (4 * p + 4))
                    alone(e)
                    with e.Fori(0, 3) as c:
                        turn = e.snap(b * 6 + c + 3 * p)
                        base = e.snap(turn * 36)
                        if p == 1:
                            e.wait_ge(conv, b * 54 + c * 18 + 54)
                            pad_tile(b * 3 + c + 3)
                        for w in range(2 * MT):
                            m, h = divmod(w, 2)
                            e.wait_ge(s_mm, base + (w + 1))
                            e.wait_ge(pv, base + (w + 1))
                            e.activation(pb[:, w % 4].rearrange("p (s l) -> p s l", s=2),
                                         ps[:, 2 * (w % 3):2 * (w % 3) + 2, 0:CH], ACT.Exp,
                                         scale=ksc[:, p, w:w + 1], bias=t_neg[:, 2 * p + h:2 * p + h + 1]).then_inc(ex, 1)
                        e.wait_ge(pv, base + (2 * MT + 4))
                        e.activation(q_v[:, p, ds(c * QC, QC)].rearrange("p (s l) -> p s l", s=2),
                                     ps[:, 6:8, 0:CH], ACT.Copy).then_inc(o_ev, 1)

            with e.Fori(0, NB) as b:
                for i, f in enumerate((front, scan_phase, back, attention)):
                    if i == 1:
                        wait_stored(e, b)
                        alone(e)
                    f(b)
                    barrier(e, b, i)

        @block.gpsimd
        def _(e):
            e.memset(hst[:], 0.0).then_inc(carry, 16)
            for s, v in ((dbus, 2), (ysum, 2), (pv, 4)):
                e.sem_inc(s, v)
            e.wait_ge(prepared, 13)

            def clear_border(v):
                e.memset(v[..., 0:1, :], 0.0)
                e.memset(v[..., HP - 1:HP, :], 0.0)
                e.memset(v[..., 1:HP - 1, 0:1], 0.0)
                return e.memset(v[..., 1:HP - 1, HP - 1:HP], 0.0)

            def stage_weights(j):
                e.tensor_tensor(w_cur, w_in[:, :, j * 128:(j + 1) * 128],
                                ones[0:CP, 0:1, None].broadcast_to([CP, CT, 128]), ALU.mult).then_inc(w_st, 1)

            def next_conv(b):
                alone(e)
                clear_border(xpad).then_inc(pad0, 1)
                for j in range(1, J):
                    e.wait_ge(in_ev, b * 9 + 3 * j)
                    stage_weights(j)

            stage_weights(0)
            next_conv(0)

            def front(b):
                o, u = column_copy(e, b, 1)
                e.tensor_tensor(o, u, ones[:, 0:1, None].broadcast_to([128, W, H]), ALU.mult).then_inc(uwh, 1)

            def scan_phase(b):
                def delta_u(g, par, k, c):
                    e.wait_ge(dp_v, g + 1)
                    e.tensor_tensor(du[:, par], dlt[:, par], u_v[:, k % 2, :, ds(pos(k, c), CH)], ALU.mult)\
                        .then_inc(dp_u, 1)

                g0 = e.snap(b * 24)
                g016 = e.snap(b * 384)
                delta_u(g0, 0, 0, 0)
                e.wait_ge(dp_u, g0 + 1)
                def delta_u_b(n, i, par):
                    e.wait_ge(b_sb, n + 1)
                    e.tensor_tensor(dbu[:, i % NH], du[:, par], bs[:, i % 2:i % 2 + 1].broadcast_to([128, J, CH]),
                                    ALU.mult).then_inc(dbus, 1)

                for i in range(3):
                    delta_u_b(g016 + i, i, 0)

                def body(k, c, par, last, nxt):
                    g = e.snap(b * 24 + (c + k * NC))
                    g16, g48 = e.snap(g * 16), e.snap(g * 48)
                    for i in range(N):
                        e.wait_ge(scan, g48 + (3 * i + 6))
                        if isinstance(c, int) and c == NC - 1:
                            alone(e)
                            e.memset(hst[:, i], 0.0).then_inc(carry, 1)
                        else:
                            e.tensor_tensor(hst[:, i], hb[:, i % NH, :, CH - 1 if k < 2 else 0], ones[:].broadcast_to([128, J]),
                                            ALU.mult).then_inc(carry, 1)
                        if i < N - 3 or nxt:
                            if i == N - 3:
                                e.wait_ge(dp_u, g + 2)
                            delta_u_b(g16 + (i + 3), i + 3, par if i < N - 3 else 1 - par)
                        if nxt and i == 12:
                            delta_u(g + 1, 1 - par, *nxt)

                walk(e, body)

            def back(b):
                e.wait_ge(x_in, b * 32 + 32)
                alone(e)
                for k in range(CT):
                    e.tensor_scalar(xn0[:, k], x_v[:, k], grs[:, 0, k:k + 1], gnb[:, 0, k:k + 1],
                                    ALU.mult, ALU.add).then_inc(xnz, 1)

            def attention(b):
                alone(e)
                for v in xp2:
                    clear_border(v)
                for p in range(PAIRS):
                    m = e.memset(kz[0:64, 2 * p + 1], 0.0)
                m.then_inc(kclr, 1)
                e.wait_ge(kclr, b + 1)
                for p in range(PAIRS):
                    wait_cv2(e, b, 3 * p + 2)
                    e.tensor_tensor(kz[64:128, 2 * p + 1], kz[64:128, 2 * p], ones[64:128, :].broadcast_to([64, L]),
                                    ALU.mult).then_inc(kzs, 1)
                    e.wait_ge(kzs, b * 4 + (2 * p + 1))
                    e.wait_ge(qsq, b * 4 + (2 * p + 2))
                    alone(e)
                    e.memset(kz[64:128, 2 * p], 0.0).then_inc(kzs, 1)
                e.wait_ge(kzs, b * 4 + 4)
                alone(e)
                stage_weights(0)
                e.wait_ge(n_mm, b * 14 + 14)
                e.wait_ge(vt_mm, b * 10 + 10)
                next_conv(b + 1)

            with e.Fori(0, NB) as b:
                for i, f in enumerate((front, scan_phase, back, attention)):
                    if i == 1:
                        wait_stored(e, b)
                        alone(e)
                    f(b)
                    barrier(e, b, i)

    return nc


def layouts(i):
    f = np.float32

    def col(a):
        return np.ascontiguousarray(np.moveaxis(a.reshape(J, 128, *a.shape[1:]), 0, 1))

    def heads(a, fill=0.0):
        o = np.full((QT * 128,) + a.shape[1:], fill, f)
        for s in range(3):
            for h in range(HEADS):
                at = ((h // 2) * 3 + (1, 2, 0)[s]) * 128 + 64 * (h % 2)
                o[at:at + HD] = a[s * C + h * HD:s * C + (h + 1) * HD]
        return o

    xp = i["L0_conv_x_proj_w"]
    w_xp = np.zeros((2, 128, DI), f)
    w_dt = np.zeros((K, 128, DI), f)
    for k in range(K):
        a = k // 2
        w_xp[k % 2, 32 * a:32 * a + 2 * N] = xp[k, R:]
        w_xp[k % 2, 64 + 32 * a:64 + 32 * a + R] = xp[k, :R]
        w_dt[k, DT0[k]:DT0[k] + R] = i["L0_conv_dt_w"][k].T
    b_dw = heads(i["L1_conv_b_dw"])
    for p in range(PAIRS):
        for h in range(2):
            b_dw[3 * p * 128 + 64 * h + HD] = 1.0
    w_pr = np.zeros((PAIRS, 128, C), f)
    t_q = np.ones((128, PAIRS), f)
    temp = i["L1_conv_temperature"].reshape(HEADS)
    hones, hind, ssel = np.zeros((128, 128), f), np.zeros((128, 2), f), np.zeros((128, 2), f)
    for h in range(HEADS):
        p, a = h // 2, 64 * (h % 2)
        w_pr[p, a:a + HD] = i["L1_conv_w_proj"].T[h * HD:(h + 1) * HD]
        t_q[a:a + 64, p] = temp[h]
        hones[a:a + 64, a:a + 64] = 1.0
        hind[a:a + 64, h % 2] = 1.0
        ssel[a + HD, h % 2] = 1.0
    qkv = heads(i["L1_conv_w_qkv"])
    return {
        "x": i["x"].reshape(NB, C, L),
        "w_in": np.moveaxis(i["L0_conv_in_proj_w"].T.reshape(CT, CP, 2 * DI), 0, 1),
        "w_xp": col(np.moveaxis(w_xp, 2, 0)),
        "w_dt": np.moveaxis(w_dt, 0, 1), "ident": np.eye(128, dtype=f),
        "a_logs": np.transpose(i["L0_conv_A_logs"].reshape(K, J, 128, N), (2, 1, 0, 3)),
        "ds": np.transpose(i["L0_conv_Ds"].reshape(K, J, 128), (2, 1, 0)),
        "w_cv": col(i["L0_conv_conv_w"].reshape(DI, 9)), "b_cv": col(i["L0_conv_conv_b"]),
        "b_dt": col(i["L0_conv_dt_b"].T), "ln_w": col(i["L0_conv_ln_w"]), "ln_b": col(i["L0_conv_ln_b"]),
        "w_out": col(i["L0_conv_out_proj_w"].T),
        "gmat": np.kron(np.eye(16, dtype=f), np.full((6, 6), 1.0 / 6, f)), "mean_m": np.full((128, 128), 1.0 / DI, f),
        "w_qkv": np.moveaxis(qkv.T.reshape(CT, CP, QT * 128), 0, 1),
        "b_qkv": heads(i["L1_conv_b_qkv"]).reshape(QT, 128).T,
        "w_dw": np.moveaxis(heads(i["L1_conv_w_dw"].reshape(3 * C, 9)).reshape(QT, 128, 9), 0, 1),
        "b_dw": b_dw.reshape(QT, 128).T, "w_pr": np.moveaxis(w_pr, 0, 1),
        "b_pr": i["L1_conv_b_proj"].reshape(CT, CP).T, "t_q": t_q,
        "t_all": np.broadcast_to(temp, (128, HEADS)), "hones": hones, "hind": hind, "ssel": ssel,
        "sel": np.tile(np.eye(2 * N, dtype=f), (3, 1)),
    }


def kernel(**inputs):
    import concourse.bacc as _bacc
    from concourse.bass_utils import run_bass_kernel_spmd as _run

    nc = _bacc.Bacc("TRN2", target_bir_lowering=False, num_devices=1)
    arrays, t = {}, {}
    for name, a in layouts({k: np.asarray(v) for k, v in inputs.items()}).items():
        a = np.ascontiguousarray(a)
        arrays[f"in_{name}"] = a
        t[name] = nc.dram_tensor(f"in_{name}", a.shape, F32, kind="ExternalInput").ap()
    out = nc.dram_tensor("out", (NB, C, L), F32, kind="ExternalOutput").ap()
    build(nc, t, out)
    r = _run(nc, [arrays], core_ids=[0])
    return r.results[0]["out"].reshape(NB, C, H, W)
```
